# Optimizing a Trainium2 kernel written in Bass

```python
import numpy as np
import jax
import jax.numpy as jnp

def _softmax(x, axis=-1):
    return jax.nn.softmax(x, axis=axis)

def _gelu(x):
    return jax.nn.gelu(x, approximate=True)

def _silu(x):
    return jax.nn.silu(x)

def _sigmoid(x):
    return jax.nn.sigmoid(x)

def _layernorm(x, axis=-1, eps=1e-05):
    m = jnp.mean(x, axis=axis, keepdims=True)
    v = jnp.var(x, axis=axis, keepdims=True)
    return (x - m) / jnp.sqrt(v + eps)

def _scatter_add(tgt, idx, src, axis=0):
    return tgt.at[idx].add(src)

def _segment_sum(src, seg, n):
    return jax.ops.segment_sum(src, seg, n)
kernel_name = 'mk_adaln_attn_ffn_d2_seqx_r4_903e4a'

def setup_inputs(seed: int=0):
    np.random.seed(seed)
    _w = jnp.asarray

    def _rec_inputs():
        import jax
        import jax.numpy as jnp
        _rk = jax.random.key(seed)
        x = -7.109e-05 + 0.9999 * jax.random.normal(jax.random.fold_in(_rk, 1), (8, 512, 256), jnp.float32)
        _lenS = 512 - jax.random.randint(jax.random.fold_in(_rk, 7), (8,), 0, max(1, 512 // 4) + 1, jnp.int32)
        _lenS2 = 512 - jax.random.randint(jax.random.fold_in(_rk, 8), (8,), 0, max(1, 512 // 4) + 1, jnp.int32)
        cond_1024 = 0.00386106 + 1.00199 * jax.random.normal(jax.random.fold_in(_rk, 11), (8, 256), jnp.float32)
        return (x, cond_1024)
    x, cond_1024 = _rec_inputs()

    def _L0_cond_setup():
        import jax, jax.numpy as jnp
        import numpy as np
        import math
        IN_F = 256
        OUT_F = 256
        B = 16
        L = 1024
        key = jax.random.key(seed)
        k1, k2, k3 = jax.random.split(key, 3)
        Efou = jax.random.normal(k1, (B, L, IN_F), dtype=jnp.float32)
        y = jax.random.normal(k2, (B, IN_F), dtype=jnp.float32)
        weight = jax.random.normal(k3, (1, OUT_F, IN_F, 1), dtype=jnp.float32)
        return {'Efou': Efou, 'y': y, 'weight': weight}
    _L0_cond_all = _L0_cond_setup()
    _L0_cond_in = {k: v for k, v in _L0_cond_all.items() if k in ('weight',)}
    del _L0_cond_all

    def _L0_attn_setup():
        import jax, jax.numpy as jnp
        import numpy as np
        HEADS, DIM_HEAD, LANDMARKS, PINV_ITERS = (8, 64, 64, 6)
        WQK_DIM = 64
        CONV_K = 33

        def moore_penrose_pinv(x, iters):
            I = jnp.eye(x.shape[-1], dtype=x.dtype)
            abs_x = jnp.abs(x)
            scale = jnp.max(abs_x.sum(-1)) * jnp.max(abs_x.sum(-2))
            z = jnp.swapaxes(x, -1, -2) / scale
            for _ in range(iters):
                xz = x @ z
                z = 0.25 * z @ (13 * I - xz @ (15 * I - xz @ (7 * I - xz)))
            return z

        def nystrom_attention(x, qkv_w, out_w, out_b, conv_w):
            b, n, d = x.shape
            h, dh, m = (HEADS, DIM_HEAD, LANDMARKS)
            scale = dh ** (-0.5)
            qkv = x @ qkv_w
            q, k, v = jnp.split(qkv, 3, axis=-1)
            split = lambda t: t.reshape(b, n, h, dh).transpose(0, 2, 1, 3)
            q, k, v = (split(q) * scale, split(k), split(v))
            l = n // m
            q_l = q.reshape(b, h, m, l, dh).mean(axis=3)
            k_l = k.reshape(b, h, m, l, dh).mean(axis=3)
            attn1 = jax.nn.softmax(jnp.einsum('bhid,bhjd->bhij', q, k_l), axis=-1)
            attn2 = jax.nn.softmax(jnp.einsum('bhid,bhjd->bhij', q_l, k_l), axis=-1)
            attn3 = jax.nn.softmax(jnp.einsum('bhid,bhjd->bhij', q_l, k), axis=-1)
            attn2_inv = moore_penrose_pinv(attn2, PINV_ITERS)
            out = attn1 @ (attn2_inv @ (attn3 @ v))
            pad = CONV_K // 2
            res = jax.lax.conv_general_dilated(v, conv_w, window_strides=(1, 1), padding=((pad, pad), (0, 0)), dimension_numbers=('NCHW', 'OIHW', 'NCHW'), feature_group_count=h)
            out = out + res
            out = out.transpose(0, 2, 1, 3).reshape(b, n, h * dh)
            return out @ out_w + out_b

        def _reference_tuple_inner(dense, adj_rows, adj_cols, adj_vals, wq, wk, wv_w, wv_b, qkv_w, out_w, out_b, conv_w):
            b, n, d = dense.shape
            xg = nystrom_attention(dense, qkv_w, out_w, out_b, conv_w)
            enc = xg[0] + dense
            q = enc @ wq
            k = enc @ wk
            scores = jnp.einsum('bid,bjd->bij', q, k) / jnp.sqrt(jnp.float32(WQK_DIM))
            data = scores[0]
            contrib = adj_vals * data[adj_rows, adj_cols]
            A_raw = jax.ops.segment_sum(contrib, adj_rows, num_segments=n)
            alpha = jax.nn.softmax(A_raw)
            value = dense @ wv_w + wv_b
            xl = alpha[:, None] * value
            wei = jax.nn.sigmoid(-xl)
            sw = wei * wei
            xo = xl * 2 * sw + 2 * enc * (1 - sw)
            return (xo, A_raw)
        key = jax.random.key(seed)
        ks = jax.random.split(key, 12)
        n, d, E = (2048, 256, 32768)
        inner = HEADS * DIM_HEAD
        s = lambda fan: (1.0 / np.sqrt(fan)).astype(np.float32) if isinstance(fan, np.ndarray) else np.float32(1.0 / np.sqrt(fan))
        return {'dense': jax.random.normal(ks[0], (1, n, d), jnp.float32), 'adj_rows': jax.random.randint(ks[1], (E,), 0, n), 'adj_cols': jax.random.randint(ks[2], (E,), 0, n), 'adj_vals': jax.random.uniform(ks[3], (E,), jnp.float32), 'wq': jax.random.normal(ks[4], (d, WQK_DIM), jnp.float32) * s(d), 'wk': jax.random.normal(ks[5], (d, WQK_DIM), jnp.float32) * s(d), 'wv_w': jax.random.normal(ks[6], (d, d), jnp.float32) * s(d), 'wv_b': jnp.zeros((d,), jnp.float32), 'qkv_w': jax.random.normal(ks[7], (d, 3 * inner), jnp.float32) * s(d), 'out_w': jax.random.normal(ks[8], (inner, d), jnp.float32) * s(inner), 'out_b': jnp.zeros((d,), jnp.float32), 'conv_w': jax.random.normal(ks[9], (HEADS, 1, CONV_K, 1), jnp.float32) * s(CONV_K)}
    _L0_attn_all = _L0_attn_setup()
    _L0_attn_in = {k: v for k, v in _L0_attn_all.items() if k in ('adj_rows', 'adj_cols', 'adj_vals', 'wq', 'wk', 'wv_w', 'wv_b', 'qkv_w', 'out_w', 'out_b', 'conv_w')}
    del _L0_attn_all

    def _L0_cond2_setup():
        import jax, jax.numpy as jnp
        import numpy as np
        import math
        N, T, D, H = (64, 128, 256, 256)
        key = jax.random.key(seed)
        k1, k2, k3, k4 = jax.random.split(key, 4)
        x = jax.random.normal(k1, (N, T, D), dtype=jnp.float32)
        h0 = jax.random.normal(k2, (N, H), dtype=jnp.float32)
        Wx = jax.random.normal(k3, (D, 4 * H), dtype=jnp.float32) / math.sqrt(D)
        Wh = jax.random.normal(k4, (H, 4 * H), dtype=jnp.float32) / math.sqrt(H)
        b = jnp.zeros((4 * H,), dtype=jnp.float32)
        return {'x': x, 'h0': h0, 'Wx': Wx, 'Wh': Wh, 'b': b}
    _L0_cond2_all = _L0_cond2_setup()
    _L0_cond2_in = {k: v for k, v in _L0_cond2_all.items() if k in ('Wx', 'Wh', 'b')}
    del _L0_cond2_all

    def _L0_ffn_setup():
        import jax, jax.numpy as jnp
        import numpy as np
        N_HEAD, N_ACTIVE, D_MODEL, D_ATTN = (16, 4, 256, 64)
        key = jax.random.key(seed)
        ks = jax.random.split(key, 12)
        s = 0.02
        B, S = (2, 1024)
        return {'x': jax.random.normal(ks[0], (B, S, D_MODEL), dtype=jnp.float32), 'Wq': jax.random.normal(ks[1], (D_MODEL, N_HEAD * D_ATTN), dtype=jnp.float32) * s, 'bq': jnp.zeros((N_HEAD * D_ATTN,), dtype=jnp.float32), 'Wk': jax.random.normal(ks[2], (D_MODEL, N_HEAD * D_ATTN), dtype=jnp.float32) * s, 'bk': jnp.zeros((N_HEAD * D_ATTN,), dtype=jnp.float32), 'Wv': jax.random.normal(ks[3], (D_MODEL, N_HEAD * D_ATTN), dtype=jnp.float32) * s, 'bv': jnp.zeros((N_HEAD * D_ATTN,), dtype=jnp.float32), 'Wr': jax.random.normal(ks[4], (D_MODEL, N_HEAD), dtype=jnp.float32) * s, 'br': jnp.zeros((N_HEAD,), dtype=jnp.float32), 'Wo': jax.random.normal(ks[5], (N_ACTIVE * D_ATTN, D_MODEL), dtype=jnp.float32) * s, 'bo': jnp.zeros((D_MODEL,), dtype=jnp.float32)}
    _L0_ffn_all = _L0_ffn_setup()
    _L0_ffn_in = {k: v for k, v in _L0_ffn_all.items() if k in ('Wq', 'bq', 'Wk', 'bk', 'Wv', 'bv', 'Wr', 'br', 'Wo', 'bo')}
    del _L0_ffn_all

    def _L1_cond_setup():
        import jax, jax.numpy as jnp
        import numpy as np
        RANK = 8
        LN_EPS = 1e-05
        key = jax.random.key(seed)
        ks = jax.random.split(key, 8)
        B, T, D = (16, 256, 256)
        A = 256
        I = 256
        OUT = D * RANK * 4
        s = 0.02
        return {'x': jax.random.normal(ks[0], (B, T, D), jnp.float32), 'ada_emb': jax.random.normal(ks[1], (B, A), jnp.float32), 'base_up': jax.random.normal(ks[2], (D, D), jnp.float32) * s, 'base_down': jax.random.normal(ks[3], (D, D), jnp.float32) * s, 'ln_gamma': jnp.ones((A,), jnp.float32), 'ln_beta': jnp.zeros((A,), jnp.float32), 'W1': jax.random.normal(ks[4], (A, I), jnp.float32) / np.sqrt(A), 'bias1': jnp.zeros((I,), jnp.float32), 'W2': jax.random.normal(ks[5], (I, OUT), jnp.float32) / np.sqrt(I), 'bias2': jnp.zeros((OUT,), jnp.float32)}
    _L1_cond_all = _L1_cond_setup()
    _L1_cond_in = {k: v for k, v in _L1_cond_all.items() if k in ('base_up', 'base_down', 'ln_gamma', 'ln_beta', 'W1', 'bias1', 'W2', 'bias2')}
    del _L1_cond_all

    def _L1_attn_setup():
        import jax, jax.numpy as jnp
        import numpy as np
        EPS = float(np.finfo(np.float32).eps)
        THETA = 10000.0

        def rms_norm(x, weight):
            var = jnp.mean(jnp.square(x), axis=-1, keepdims=True)
            return x * jax.lax.rsqrt(var + EPS) * weight

        def rotate_half(x):
            x1 = x[..., ::2]
            x2 = x[..., 1::2]
            return jnp.stack((-x2, x1), axis=-1).reshape(x.shape)

        def apply_rope(t):
            d = t.shape[-1]
            n = t.shape[-2]
            inv_freq = 1.0 / THETA ** (jnp.arange(0, d, 2, dtype=jnp.float32) / d)
            freqs = jnp.arange(n, dtype=jnp.float32)[:, None] * inv_freq[None, :]
            freqs = jnp.repeat(freqs, 2, axis=-1)
            cos = jnp.cos(freqs).astype(t.dtype)
            sin = jnp.sin(freqs).astype(t.dtype)
            return t * cos + rotate_half(t) * sin
        key = jax.random.key(seed)
        k1, k2, k3, k4 = jax.random.split(key, 4)
        b, n, dim = (4, 512, 256)
        heads, dim_head, n_pm = (16, 64, 4)
        dim_inner = heads * dim_head
        return {'x': jax.random.normal(k1, (b, n, dim), dtype=jnp.float32), 'norm_weight': jnp.ones((dim,), dtype=jnp.float32), 'w_qkv': jax.random.normal(k2, (3 * dim_inner, dim), dtype=jnp.float32) * dim ** (-0.5), 'w_out': jax.random.normal(k3, (dim, dim_inner), dtype=jnp.float32) * dim_inner ** (-0.5), 'persist_mem': jax.random.normal(k4, (heads, n_pm, dim_head), dtype=jnp.float32)}
    _L1_attn_all = _L1_attn_setup()
    _L1_attn_in = {k: v for k, v in _L1_attn_all.items() if k in ('norm_weight', 'w_qkv', 'w_out', 'persist_mem')}
    del _L1_attn_all

    def _L1_cond2_setup():
        import jax, jax.numpy as jnp
        import numpy as np
        N, T, D, H = (128, 128, 256, 256)
        key = jax.random.key(seed)
        k1, k2, k3, k4 = jax.random.split(key, 4)
        x = jax.random.normal(k1, (N, T, D), dtype=jnp.float32)
        h0 = jax.random.normal(k2, (N, H), dtype=jnp.float32)
        Wx = jax.random.normal(k3, (D, H), dtype=jnp.float32) / np.sqrt(D)
        Wh = jax.random.normal(k4, (H, H), dtype=jnp.float32) / np.sqrt(H)
        b = jnp.zeros((H,), dtype=jnp.float32)
        return {'x': x, 'h0': h0, 'Wx': Wx, 'Wh': Wh, 'b': b}
    _L1_cond2_all = _L1_cond2_setup()
    _L1_cond2_in = {k: v for k, v in _L1_cond2_all.items() if k in ('Wx', 'Wh', 'b')}
    del _L1_cond2_all

    def _L1_ffn_setup():
        import jax, jax.numpy as jnp
        import numpy as np
        B, S, D = (2, 512, 256)
        I = 128
        E = 16
        TOP_K = 2

        def _mlp(x, wg, wu, wd):
            return jnp.einsum('bsi,id->bsd', jax.nn.silu(x @ wg) * (x @ wu), wd)
        key = jax.random.key(seed)
        ks = jax.random.split(key, 10)
        sc_d = 1.0 / np.sqrt(D)
        sc_i = 1.0 / np.sqrt(I)
        return {'x': jax.random.normal(ks[0], (B, S, D), dtype=jnp.float32), 'gate_w': jax.random.normal(ks[1], (D, E), dtype=jnp.float32) * sc_d, 'gate_b': jnp.zeros((E,), dtype=jnp.float32), 'shared_wg': jax.random.normal(ks[2], (D, I), dtype=jnp.float32) * sc_d, 'shared_wu': jax.random.normal(ks[3], (D, I), dtype=jnp.float32) * sc_d, 'shared_wd': jax.random.normal(ks[4], (I, D), dtype=jnp.float32) * sc_i, 'experts_wg': jax.random.normal(ks[5], (E, D, I), dtype=jnp.float32) * sc_d, 'experts_wu': jax.random.normal(ks[6], (E, D, I), dtype=jnp.float32) * sc_d, 'experts_wd': jax.random.normal(ks[7], (E, I, D), dtype=jnp.float32) * sc_i}
    _L1_ffn_all = _L1_ffn_setup()
    _L1_ffn_in = {k: v for k, v in _L1_ffn_all.items() if k in ('gate_w', 'gate_b', 'shared_wg', 'shared_wu', 'shared_wd', 'experts_wg', 'experts_wu', 'experts_wd')}
    del _L1_ffn_all
    return {'x': x, 'cond_1024': cond_1024, 'L0_cond_weight': _L0_cond_in['weight'], 'L0_attn_adj_rows': _L0_attn_in['adj_rows'], 'L0_attn_adj_cols': _L0_attn_in['adj_cols'], 'L0_attn_adj_vals': _L0_attn_in['adj_vals'], 'L0_attn_wq': _L0_attn_in['wq'], 'L0_attn_wk': _L0_attn_in['wk'], 'L0_attn_wv_w': _L0_attn_in['wv_w'], 'L0_attn_wv_b': _L0_attn_in['wv_b'], 'L0_attn_qkv_w': _L0_attn_in['qkv_w'], 'L0_attn_out_w': _L0_attn_in['out_w'], 'L0_attn_out_b': _L0_attn_in['out_b'], 'L0_attn_conv_w': _L0_attn_in['conv_w'], 'L0_cond2_Wx': _L0_cond2_in['Wx'], 'L0_cond2_Wh': _L0_cond2_in['Wh'], 'L0_cond2_b': _L0_cond2_in['b'], 'L0_ffn_Wq': _L0_ffn_in['Wq'], 'L0_ffn_bq': _L0_ffn_in['bq'], 'L0_ffn_Wk': _L0_ffn_in['Wk'], 'L0_ffn_bk': _L0_ffn_in['bk'], 'L0_ffn_Wv': _L0_ffn_in['Wv'], 'L0_ffn_bv': _L0_ffn_in['bv'], 'L0_ffn_Wr': _L0_ffn_in['Wr'], 'L0_ffn_br': _L0_ffn_in['br'], 'L0_ffn_Wo': _L0_ffn_in['Wo'], 'L0_ffn_bo': _L0_ffn_in['bo'], 'L1_cond_base_up': _L1_cond_in['base_up'], 'L1_cond_base_down': _L1_cond_in['base_down'], 'L1_cond_ln_gamma': _L1_cond_in['ln_gamma'], 'L1_cond_ln_beta': _L1_cond_in['ln_beta'], 'L1_cond_W1': _L1_cond_in['W1'], 'L1_cond_bias1': _L1_cond_in['bias1'], 'L1_cond_W2': _L1_cond_in['W2'], 'L1_cond_bias2': _L1_cond_in['bias2'], 'L1_attn_norm_weight': _L1_attn_in['norm_weight'], 'L1_attn_w_qkv': _L1_attn_in['w_qkv'], 'L1_attn_w_out': _L1_attn_in['w_out'], 'L1_attn_persist_mem': _L1_attn_in['persist_mem'], 'L1_cond2_Wx': _L1_cond2_in['Wx'], 'L1_cond2_Wh': _L1_cond2_in['Wh'], 'L1_cond2_b': _L1_cond2_in['b'], 'L1_ffn_gate_w': _L1_ffn_in['gate_w'], 'L1_ffn_gate_b': _L1_ffn_in['gate_b'], 'L1_ffn_shared_wg': _L1_ffn_in['shared_wg'], 'L1_ffn_shared_wu': _L1_ffn_in['shared_wu'], 'L1_ffn_shared_wd': _L1_ffn_in['shared_wd'], 'L1_ffn_experts_wg': _L1_ffn_in['experts_wg'], 'L1_ffn_experts_wu': _L1_ffn_in['experts_wu'], 'L1_ffn_experts_wd': _L1_ffn_in['experts_wd']}

def reference(x, cond_1024, L0_cond_weight, L0_attn_adj_rows, L0_attn_adj_cols, L0_attn_adj_vals, L0_attn_wq, L0_attn_wk, L0_attn_wv_w, L0_attn_wv_b, L0_attn_qkv_w, L0_attn_out_w, L0_attn_out_b, L0_attn_conv_w, L0_cond2_Wx, L0_cond2_Wh, L0_cond2_b, L0_ffn_Wq, L0_ffn_bq, L0_ffn_Wk, L0_ffn_bk, L0_ffn_Wv, L0_ffn_bv, L0_ffn_Wr, L0_ffn_br, L0_ffn_Wo, L0_ffn_bo, L1_cond_base_up, L1_cond_base_down, L1_cond_ln_gamma, L1_cond_ln_beta, L1_cond_W1, L1_cond_bias1, L1_cond_W2, L1_cond_bias2, L1_attn_norm_weight, L1_attn_w_qkv, L1_attn_w_out, L1_attn_persist_mem, L1_cond2_Wx, L1_cond2_Wh, L1_cond2_b, L1_ffn_gate_w, L1_ffn_gate_b, L1_ffn_shared_wg, L1_ffn_shared_wu, L1_ffn_shared_wd, L1_ffn_experts_wg, L1_ffn_experts_wu, L1_ffn_experts_wd):
    import jax
    import jax.numpy as jnp

    def _L0_cond_ref(Efou, y, weight):
        import jax, jax.numpy as jnp
        import numpy as np
        import math
        IN_F = 256
        OUT_F = 256
        B = 16
        L = 1024
        b, img_size, in_f = Efou.shape
        out_f = weight.shape[1]
        scale = 1.0 / math.sqrt(in_f)
        w = scale * weight[:, :, :, 0] * y[:, None, :]
        dnorm = jax.lax.rsqrt(jnp.sum(w * w, axis=2, keepdims=True) + 1e-08)
        w = w * dnorm
        E = Efou.reshape(b, in_f, img_size)
        x = jnp.einsum('boi,bil->bol', w, E)
        return x.reshape(b, img_size, out_f)

    def _L0_attn_ref(dense, adj_rows, adj_cols, adj_vals, wq, wk, wv_w, wv_b, qkv_w, out_w, out_b, conv_w):
        import jax, jax.numpy as jnp
        import numpy as np
        HEADS, DIM_HEAD, LANDMARKS, PINV_ITERS = (8, 64, 64, 6)
        WQK_DIM = 64
        CONV_K = 33

        def moore_penrose_pinv(x, iters):
            I = jnp.eye(x.shape[-1], dtype=x.dtype)
            abs_x = jnp.abs(x)
            scale = jnp.max(abs_x.sum(-1)) * jnp.max(abs_x.sum(-2))
            z = jnp.swapaxes(x, -1, -2) / scale
            for _ in range(iters):
                xz = x @ z
                z = 0.25 * z @ (13 * I - xz @ (15 * I - xz @ (7 * I - xz)))
            return z

        def nystrom_attention(x, qkv_w, out_w, out_b, conv_w):
            b, n, d = x.shape
            h, dh, m = (HEADS, DIM_HEAD, LANDMARKS)
            scale = dh ** (-0.5)
            qkv = x @ qkv_w
            q, k, v = jnp.split(qkv, 3, axis=-1)
            split = lambda t: t.reshape(b, n, h, dh).transpose(0, 2, 1, 3)
            q, k, v = (split(q) * scale, split(k), split(v))
            l = n // m
            q_l = q.reshape(b, h, m, l, dh).mean(axis=3)
            k_l = k.reshape(b, h, m, l, dh).mean(axis=3)
            attn1 = jax.nn.softmax(jnp.einsum('bhid,bhjd->bhij', q, k_l), axis=-1)
            attn2 = jax.nn.softmax(jnp.einsum('bhid,bhjd->bhij', q_l, k_l), axis=-1)
            attn3 = jax.nn.softmax(jnp.einsum('bhid,bhjd->bhij', q_l, k), axis=-1)
            attn2_inv = moore_penrose_pinv(attn2, PINV_ITERS)
            out = attn1 @ (attn2_inv @ (attn3 @ v))
            pad = CONV_K // 2
            res = jax.lax.conv_general_dilated(v, conv_w, window_strides=(1, 1), padding=((pad, pad), (0, 0)), dimension_numbers=('NCHW', 'OIHW', 'NCHW'), feature_group_count=h)
            out = out + res
            out = out.transpose(0, 2, 1, 3).reshape(b, n, h * dh)
            return out @ out_w + out_b

        def _reference_tuple_inner(dense, adj_rows, adj_cols, adj_vals, wq, wk, wv_w, wv_b, qkv_w, out_w, out_b, conv_w):
            b, n, d = dense.shape
            xg = nystrom_attention(dense, qkv_w, out_w, out_b, conv_w)
            enc = xg[0] + dense
            q = enc @ wq
            k = enc @ wk
            scores = jnp.einsum('bid,bjd->bij', q, k) / jnp.sqrt(jnp.float32(WQK_DIM))
            data = scores[0]
            contrib = adj_vals * data[adj_rows, adj_cols]
            A_raw = jax.ops.segment_sum(contrib, adj_rows, num_segments=n)
            alpha = jax.nn.softmax(A_raw)
            value = dense @ wv_w + wv_b
            xl = alpha[:, None] * value
            wei = jax.nn.sigmoid(-xl)
            sw = wei * wei
            xo = xl * 2 * sw + 2 * enc * (1 - sw)
            return (xo, A_raw)
        return _reference_tuple_inner(dense, adj_rows, adj_cols, adj_vals, wq, wk, wv_w, wv_b, qkv_w, out_w, out_b, conv_w)[0]

    def _L0_cond2_ref(x, h0, Wx, Wh, b):
        import jax, jax.numpy as jnp
        import numpy as np
        import math
        N, T, D, H = (64, 128, 256, 256)
        Hdim = h0.shape[1]
        xW = jnp.einsum('ntd,dg->ntg', x, Wx) + b

        def step(carry, xw_t):
            prev_h, prev_c = carry
            a = xw_t + prev_h @ Wh
            i = jax.nn.sigmoid(a[:, :Hdim])
            f = jax.nn.sigmoid(a[:, Hdim:2 * Hdim])
            o = jax.nn.sigmoid(a[:, 2 * Hdim:3 * Hdim])
            g = jnp.tanh(a[:, 3 * Hdim:])
            next_c = f * prev_c + i * g
            next_h = o * jnp.tanh(next_c)
            return ((next_h, next_c), next_h)
        c0 = jnp.zeros_like(h0)
        _, hs = jax.lax.scan(step, (h0, c0), jnp.swapaxes(xW, 0, 1))
        return jnp.swapaxes(hs, 0, 1)

    def _L0_ffn_ref(x, Wq, bq, Wk, bk, Wv, bv, Wr, br, Wo, bo):
        import jax, jax.numpy as jnp
        import numpy as np
        N_HEAD, N_ACTIVE, D_MODEL, D_ATTN = (16, 4, 256, 64)
        B, S, D = x.shape
        H, K, dh = (N_HEAD, N_ACTIVE, D_ATTN)
        dist = jax.nn.softmax(jnp.mean(x @ Wr + br, axis=1), axis=-1)
        top_vals, top_idx = jax.lax.top_k(dist, K)
        sparse = jnp.zeros_like(dist).at[jnp.arange(B)[:, None], top_idx].set(top_vals)
        gates_all = jax.nn.softmax(sparse, axis=1)
        g = jnp.take_along_axis(gates_all, top_idx, axis=1)[:, :, None, None]

        def proj(W, b):
            return (x @ W + b).reshape(B, S, H, dh).transpose(0, 2, 1, 3)
        Q, Kt, V = (proj(Wq, bq), proj(Wk, bk), proj(Wv, bv))
        idx = top_idx[:, :, None, None]
        Qk = jnp.take_along_axis(Q, idx, axis=1) * g
        Kk = jnp.take_along_axis(Kt, idx, axis=1) * g
        Vk = jnp.take_along_axis(V, idx, axis=1) * g
        scores = jnp.einsum('bksd,bktd->bkst', Qk, Kk) / jnp.sqrt(jnp.float32(dh))
        attn = jax.nn.softmax(scores, axis=-1)
        out = jnp.einsum('bkst,bktd->bksd', attn, Vk)
        out = out.transpose(0, 2, 1, 3).reshape(B, S, K * dh)
        return out @ Wo + bo

    def _L1_cond_ref(x, ada_emb, base_up, base_down, ln_gamma, ln_beta, W1, bias1, W2, bias2):
        import jax, jax.numpy as jnp
        import numpy as np
        RANK = 8
        LN_EPS = 1e-05
        B, T, D = x.shape
        R = RANK
        mu = jnp.mean(ada_emb, axis=-1, keepdims=True)
        var = jnp.mean(jnp.square(ada_emb - mu), axis=-1, keepdims=True)
        c = (ada_emb - mu) / jnp.sqrt(var + LN_EPS) * ln_gamma + ln_beta
        h = jax.nn.gelu(c @ W1 + bias1, approximate=False)
        w = h @ W2 + bias2
        a1, b1, a2, b2 = [t.reshape(B, D, R) for t in jnp.split(w, 4, axis=-1)]
        u = jnp.einsum('btd,bdr->btr', x, a2)
        mid = jnp.einsum('btd,dl->btl', x, base_down) + jnp.einsum('btr,blr->btl', u, b2)
        mid = jax.nn.gelu(mid, approximate=False)
        v = jnp.einsum('blr,btl->btr', b1, mid)
        out = jnp.einsum('btl,kl->btk', mid, base_up) + jnp.einsum('bkr,btr->btk', a1, v)
        return x + out

    def _L1_attn_ref(x, norm_weight, w_qkv, w_out, persist_mem):
        import jax, jax.numpy as jnp
        import numpy as np
        EPS = float(np.finfo(np.float32).eps)
        THETA = 10000.0

        def rms_norm(x, weight):
            var = jnp.mean(jnp.square(x), axis=-1, keepdims=True)
            return x * jax.lax.rsqrt(var + EPS) * weight

        def rotate_half(x):
            x1 = x[..., ::2]
            x2 = x[..., 1::2]
            return jnp.stack((-x2, x1), axis=-1).reshape(x.shape)

        def apply_rope(t):
            d = t.shape[-1]
            n = t.shape[-2]
            inv_freq = 1.0 / THETA ** (jnp.arange(0, d, 2, dtype=jnp.float32) / d)
            freqs = jnp.arange(n, dtype=jnp.float32)[:, None] * inv_freq[None, :]
            freqs = jnp.repeat(freqs, 2, axis=-1)
            cos = jnp.cos(freqs).astype(t.dtype)
            sin = jnp.sin(freqs).astype(t.dtype)
            return t * cos + rotate_half(t) * sin
        b, n, _ = x.shape
        heads, n_pm, dim_head = persist_mem.shape
        h = rms_norm(x, norm_weight)
        qkv = h @ w_qkv.T
        q, k, v = jnp.split(qkv, 3, axis=-1)

        def split_heads(t):
            return t.reshape(b, n, heads, dim_head).transpose(0, 2, 1, 3)
        q, k, v = (split_heads(q), split_heads(k), split_heads(v))
        q = apply_rope(q)
        k = apply_rope(k)
        pm = jnp.broadcast_to(persist_mem[None], (b, heads, n_pm, dim_head))
        k = jnp.concatenate([pm, k], axis=2)
        v = jnp.concatenate([pm, v], axis=2)
        kv_len = k.shape[2]
        scale = dim_head ** (-0.5)
        scores = jnp.einsum('bhid,bhjd->bhij', q, k) * scale
        i = jnp.arange(n)[:, None]
        j = jnp.arange(kv_len)[None, :]
        causal = j <= i + (kv_len - n)
        scores = jnp.where(causal, scores, jnp.finfo(scores.dtype).min)
        attn = jax.nn.softmax(scores, axis=-1)
        out = jnp.einsum('bhij,bhjd->bhid', attn, v)
        out = out.transpose(0, 2, 1, 3).reshape(b, n, heads * dim_head)
        return out @ w_out.T

    def _L1_cond2_ref(x, h0, Wx, Wh, b):
        import jax, jax.numpy as jnp
        import numpy as np
        N, T, D, H = (128, 128, 256, 256)
        xW = jnp.einsum('ntd,dh->nth', x, Wx) + b

        def step(h_prev, xw_t):
            h_next = jnp.tanh(xw_t + h_prev @ Wh)
            return (h_next, h_next)
        _, hs = jax.lax.scan(step, h0, jnp.swapaxes(xW, 0, 1))
        return jnp.swapaxes(hs, 0, 1)

    def _L1_ffn_ref(x, gate_w, gate_b, shared_wg, shared_wu, shared_wd, experts_wg, experts_wu, experts_wd):
        import jax, jax.numpy as jnp
        import numpy as np
        B, S, D = (2, 512, 256)
        I = 128
        E = 16
        TOP_K = 2

        def _mlp(x, wg, wu, wd):
            return jnp.einsum('bsi,id->bsd', jax.nn.silu(x @ wg) * (x @ wu), wd)
        router_logits = jax.nn.sigmoid(x @ gate_w + gate_b)
        expert_values, expert_indices = jax.lax.top_k(router_logits, k=TOP_K)
        expert_values = expert_values / jnp.sum(expert_values, axis=-1, keepdims=True)
        hg = jnp.einsum('bsd,edi->bsei', x, experts_wg)
        hu = jnp.einsum('bsd,edi->bsei', x, experts_wu)
        all_outputs = jnp.einsum('bsei,eid->bsed', jax.nn.silu(hg) * hu, experts_wd)
        selected = jnp.take_along_axis(all_outputs, expert_indices[..., None], axis=2)
        expert_weighted = jnp.sum(expert_values[..., None] * selected, axis=2)
        return x + _mlp(x, shared_wg, shared_wu, shared_wd) + expert_weighted
    x = x + _L0_attn_ref(_L0_cond_ref(x, cond_1024, L0_cond_weight), L0_attn_adj_rows, L0_attn_adj_cols, L0_attn_adj_vals, L0_attn_wq, L0_attn_wk, L0_attn_wv_w, L0_attn_wv_b, L0_attn_qkv_w, L0_attn_out_w, L0_attn_out_b, L0_attn_conv_w)
    x = x + _L0_ffn_ref(_L0_cond2_ref(x, cond_1024, L0_cond2_Wx, L0_cond2_Wh, L0_cond2_b), L0_ffn_Wq, L0_ffn_bq, L0_ffn_Wk, L0_ffn_bk, L0_ffn_Wv, L0_ffn_bv, L0_ffn_Wr, L0_ffn_br, L0_ffn_Wo, L0_ffn_bo)
    x = x + _L1_attn_ref(_L1_cond_ref(x, cond_1024, L1_cond_base_up, L1_cond_base_down, L1_cond_ln_gamma, L1_cond_ln_beta, L1_cond_W1, L1_cond_bias1, L1_cond_W2, L1_cond_bias2), L1_attn_norm_weight, L1_attn_w_qkv, L1_attn_w_out, L1_attn_persist_mem)
    x = x + _L1_ffn_ref(_L1_cond2_ref(x, cond_1024, L1_cond2_Wx, L1_cond2_Wh, L1_cond2_b), L1_ffn_gate_w, L1_ffn_gate_b, L1_ffn_shared_wg, L1_ffn_shared_wu, L1_ffn_shared_wd, L1_ffn_experts_wg, L1_ffn_experts_wu, L1_ffn_experts_wd)
    return x

_drawn_inputs = setup_inputs


def setup_inputs(seed=0):
    import zlib

    import numpy as np

    out = dict(_drawn_inputs(seed))
    spreads = {'L0_attn_wv_b': (0.0, 2.0),
     'L0_attn_out_b': (0.0, 0.1),
     'L0_cond2_b': (0.0, 2.0),
     'L0_ffn_bq': (0.0, 2.0),
     'L0_ffn_bk': (0.0, 2.0),
     'L0_ffn_bv': (0.0, 0.8),
     'L0_ffn_br': (0.0, 0.8),
     'L0_ffn_bo': (0.0, 0.1),
     'L1_cond_ln_gamma': (1.0, 0.2),
     'L1_cond_ln_beta': (0.0, 0.1),
     'L1_cond_bias1': (0.0, 0.1),
     'L1_cond_bias2': (0.0, 0.1),
     'L1_attn_norm_weight': (1.0, 0.2),
     'L1_cond2_b': (0.0, 0.1),
     'L1_ffn_gate_b': (0.0, 0.1)}
    factors = {'L0_attn_adj_vals': 4.176,
     'L0_attn_wq': 2.857,
     'L0_cond2_Wx': 8.0,
     'L0_cond2_Wh': 8.0,
     'L0_ffn_Wq': 200.0,
     'L0_ffn_Wk': 200.0,
     'L0_ffn_Wv': 32.489,
     'L0_ffn_Wr': 8.0,
     'L0_ffn_Wo': 8.0,
     'L1_cond_base_up': 5.726,
     'L1_cond_base_down': 7.706}
    for name, (base, spread) in spreads.items():
        noise = np.random.default_rng([zlib.crc32(name.encode()), seed]).standard_normal(out[name].shape)
        drawn = base * np.exp(spread * noise) if base else spread * noise
        out[name] = jnp.asarray(drawn.astype(out[name].dtype))
    for name, factor in factors.items():
        out[name] = (out[name] * factor).astype(out[name].dtype)
    return out
```

```python
import concourse.bass as bass
from concourse import mybir
from contextlib import ExitStack, contextmanager
import numpy as np
P=128
F32=mybir.dt.float32; F16=mybir.dt.float16; BF16=mybir.dt.bfloat16; U32=mybir.dt.uint32
ALU = mybir.AluOpType
ACT = mybir.ActivationFunctionType
X_AX=mybir.AxisListType.X
NB,T,D,NH=8,512,256,256
C=16
I=128; NE=16; NX=NE+1
HEADS,DH,PM=16,64,4
PAIRS=HEADS//2
KV=T+PM
INNER_=HEADS*DH
MASKED=-1e30
RANK=8
H0,K0=16,4
LH,LMK,TAPS,PINV=8,64,33,6
LI=LH*DH; LP=LH//2; GROUP=T//LMK; EDGES=32768; ECH=EDGES//P; EGRP=4; WIN=P+TAPS-1
CPG=EGRP*P
NGRP=EDGES//CPG
PRE=4



@contextmanager
def semaphores(nc, stage):
    taken=[]
    def take(name):
        taken.append(nc.alloc_semaphore(name=stage+name))
        return taken[-1]
    yield take
    nc.clear_and_free_semaphores(taken)
    nc.all_engine_barrier()


def make_ident(nc, ident):
    with ExitStack() as ctx:
        s=ctx.enter_context(semaphores(nc,"ident_"))("step")
        with nc.Block() as blk:
            @blk.gpsimd
            def _(pool):
                nc.gpsimd.memset(ident[:,:],0.0).then_inc(s,1)
                pool.wait_ge(s,1)
                nc.gpsimd.affine_select(out=ident[:,:],in_=ident[:,:],compare_op=ALU.not_equal,fill=1.0,base=0,pattern=[[-1,P]],channel_multiplier=1).then_inc(s,1)
                pool.wait_ge(s,2)


def dense_stage(nc, XT, HT, x, xT, condT, wT_in, h0T, loads):
    with ExitStack() as ctx:
        sb=lambda n,s,d=F32: ctx.enter_context(nc.sbuf_tensor("mod_"+n,s,d))
        sem=ctx.enter_context(semaphores(nc,"mod_"))
        W=sb("W",[P,2,D]); xn=sb("xn",[P,2,2,2*D]); wy=sb("wy",[P,2,2,D]); sq=sb("sq",[P,2,D]); rt=sb("rt",[P,D]); dn=sb("dn",[P,D]); eps=sb("eps",[P,1]); ones=sb("ones",[P,P]); ysc=sb("ysc",[P,2,NB])
        ps_n=ctx.enter_context(nc.psum_tensor("mod_ps_n",[P,512],F32)); ps_d=ctx.enter_context(nc.psum_tensor("mod_ps_d",[P,2,2,512],F32))
        x_in=[sem(f"x_in{i}") for i in range(2)]; w_in,h_in,xt_in,rest_in,const,yscaled,modded,squared,summed,rooted,inverted,mixed,kept=[sem(n) for n in "w_in,h_in,xt_in,rest_in,const,yscaled,modded,squared,summed,rooted,inverted,mixed,kept".split(",")]
        block=ctx.enter_context(nc.Block())
        @block.sync
        def _(sp):
            ctx.enter_context(nc.allow_non_contiguous_dma(reason="a few small vectors"))
            sp.dma_start(h0T[:,:,:],condT).then_inc(h_in,16)
            sp.dma_start(W[:,:,:],wT_in.rearrange("(k p) o -> p k o",p=P)).then_inc(w_in,16)
            for b in range(NB):
                if b>=2: sp.wait_ge(mixed,b-1)
                sp.dma_start(xn[:,b%2],x[b].rearrange("(k i h) f -> i k (h f)",k=2,h=2)).then_inc(x_in[b%2],16)
            sp.dma_start(XT[:,:,:,:],xT).then_inc(xt_in,16)
            for dst,src in loads: sp.dma_start(dst,src).then_inc(rest_in,16)
            sp.wait_ge(xt_in,16); sp.wait_ge(rest_in,16*len(loads))
        @block.gpsimd
        def _(pool):
            nc.gpsimd.memset(ones[:,:],1.0).then_inc(const,1)
            nc.gpsimd.memset(eps[:,:],1e-8).then_inc(const,1)
        @block.vector
        def _(dve):
            dve.wait_ge(h_in,16); dve.wait_ge(w_in,16)
            nc.vector.tensor_scalar(ysc[:,:,:],h0T[:,:,:],D**-0.5,None,ALU.mult).then_inc(yscaled,1)
            dve.wait_ge(yscaled,1)
            for b in range(NB):
                if b>=2: dve.wait_ge(mixed,b-1)
                for k in range(2): nc.vector.tensor_scalar(wy[:,b%2,k],W[:,k],ysc[:,k,b:b+1],None,ALU.mult).then_inc(modded,1)
                dve.wait_ge(modded,2*b+2); dve.wait_ge(summed,b)
                nc.vector.tensor_tensor(sq[:,:,:],wy[:,b%2],wy[:,b%2],ALU.mult).then_inc(squared,1)
                dve.wait_ge(rooted,b+1)
                nc.vector.reciprocal(dn[:,:],rt[:,:]).then_inc(inverted,1)
                dve.wait_ge(mixed,b+1); dve.wait_ge(inverted,b+1)
                for k in range(2):
                    for h in range(2):
                        i=nc.vector.tensor_tensor(HT[:,k,b,h:T:2],ps_d[:,b%2,k,h*D:(h+1)*D],dn[:,:],ALU.mult)
                i.then_inc(kept,1)
        @block.scalar
        def _(act):
            act.wait_ge(const,2)
            for b in range(NB):
                act.wait_ge(summed,b+1)
                if b: act.wait_ge(inverted,b)
                nc.scalar.activation(rt[:,:],ps_n[:,0:D],ACT.Sqrt,bias=eps[:,0:1]).then_inc(rooted,1)
        @block.tensor
        def _(pe):
            pe.wait_ge(const,2)
            for b in range(NB):
                pe.wait_ge(squared,b+1)
                if b: pe.wait_ge(rooted,b)
                for k in range(2): i=nc.tensor.matmul(ps_n[:,0:D],ones[:,:],sq[:,k],start=(k==0),stop=(k==1))
                i.then_inc(summed,1)
                pe.wait_ge(x_in[b%2],16*(b//2+1))
                if b>=2: pe.wait_ge(kept,b-1)
                for f in range(2):
                    for h in range(2):
                        for k in range(2): i=nc.tensor.matmul(ps_d[:,b%2,f,h*D:(h+1)*D],xn[:,b%2,k,h*D+f*P:h*D+(f+1)*P],wy[:,b%2,k],start=(k==0),stop=(k==1))
                i.then_inc(mixed,1)


def nystrom_stage(nc, HT, wqkv, out_w, out_b, conv, xg, ident, taps_dram):
    with ExitStack() as ctx:
        sb=lambda n,s,d=F32: ctx.enter_context(nc.sbuf_tensor("lm_"+n,s,d))
        v=sb("v",[P,4,LI]); A1T=sb("A1T",[P,LP,T]); A3T=sb("A3T",[P,4,LP,P]); A2b=sb("A2b",[P,LP,P]); i3=sb("i3",[P,LP]); rs=sb("rs",[P,1]); bd=sb("bd",[P,P]); taps=sb("taps",[P,LH,WIN])
        with ExitStack() as c1:
            sb1=lambda n,s,d=F32: c1.enter_context(nc.sbuf_tensor("land_"+n,s,d))
            sem1=c1.enter_context(semaphores(nc,"land_"))
            lm=sb1("mean",[P,2,NB*LMK]); qbd=sb1("qbd",[P,LP,NB,P]); kl=sb1("kl",[P,LP,NB*LMK]); klbd=sb1("klbd",[P,LP,P])
            qT=sb1("qT",[P,LP,T]); kT=sb1("kT",[P,LP,T]); A1=sb1("A1",[P,4,LI]); A2=sb1("A2",[P,LP,NB*LMK]); A3=sb1("A3",[P,LP,T])
            mx=sb1("mx",[P,3,LP,8]); s1=sb1("s1",[P,2,LP,8]); cm=sb1("cm",[P,LP+2]); m2=sb1("m2",[1,8]); line=sb1("line",[LH,P-1+WIN]); one=sb1("one",[1,P])
            A=c1.enter_context(nc.psum_tensor("land_A",[P,4,512],F32)); B=c1.enter_context(nc.psum_tensor("land_B",[P,4,512],F32))
            const,dv,ac,st,conv_in,line_out,taps_in,zeroed=[sem1(n) for n in "const,dv,ac,st,conv_in,line_out,taps_in,zeroed".split(",")]
            block=c1.enter_context(nc.Block())
            @block.gpsimd
            def _(pool):
                nc.gpsimd.memset(line[:,:],0.0).then_inc(zeroed,1)
                nc.gpsimd.memset(one[:,:],1.0).then_inc(const,1)
                nc.gpsimd.memset(qbd[:,:,:,:],0.0).then_inc(const,1)
                nc.gpsimd.memset(klbd[:,:,:],0.0).then_inc(const,1)
                nc.gpsimd.memset(bd[:,:],0.0).then_inc(const,1)
                nc.gpsimd.memset(A2b[:,:,:],0.0).then_inc(const,1)
                pool.wait_ge(const,5)
                for h in range(2): nc.gpsimd.memset(bd[h*DH:(h+1)*DH,h*DH:(h+1)*DH],1.0).then_inc(const,1)
            @block.sync
            def _(sp):
                sp.wait_ge(zeroed,1)
                sp.dma_start(line[:,P-1:P-1+TAPS],conv).then_inc(conv_in,16)
                sp.wait_ge(conv_in,16)
                sp.dma_start(taps_dram,line[:,:].rearrange("h (a l) -> h a l",a=1).broadcast_to([LH,P,P-1+WIN])).then_inc(line_out,16)
                sp.wait_ge(line_out,16)
                L=P-1+WIN
                sp.dma_start(taps[:,:,:],bass.AP(taps_dram.tensor,P-1,[[L-1,P],[P*L,LH],[1,WIN]])).then_inc(taps_in,16)
                sp.wait_ge(taps_in,16)
            @block.vector
            def _(dve):
                c_=[0]
                def step(i):
                    c_[0]+=1; i.then_inc(dv,1); dve.wait_ge(dv,c_[0])
                for k in range(2): i=nc.vector.tensor_reduce(out=lm[:,k,:],in_=HT[:,k,:,:].rearrange("p b (m g) -> p (b m) g",g=GROUP),axis=X_AX,op=ALU.add)
                step(i)
                dve.wait_ge(const,5); dve.wait_ge(st,2)
                nc.vector.tensor_scalar(kl[:,:,:],B[:,:,:],1.0/GROUP,None,ALU.mult)
                for h in range(2): i=nc.vector.tensor_scalar(klbd[h*DH:(h+1)*DH,:,h*DH:(h+1)*DH],B[h*DH:(h+1)*DH,:,0:LMK],1.0/GROUP,None,ALU.mult)
                step(i)
                dve.wait_ge(st,4)
                step(nc.vector.tensor_copy(kT[:,:,:],B[:,:,:]))
                def soft(ps,dst,w,done):
                    r=lambda a: a.rearrange("p j (b m) -> p j b m",m=LMK)
                    for j in range(LP): i=nc.vector.tensor_reduce(out=mx[:,w,j],in_=ps[:,j].rearrange("p (b m) -> p b m",m=LMK),axis=X_AX,op=ALU.max)
                    step(i)
                    for j in range(LP): i=nc.vector.tensor_tensor(dst[:,j].rearrange("p (b m) -> p b m",m=LMK),ps[:,j].rearrange("p (b m) -> p b m",m=LMK),mx[:,w,j:j+1].rearrange("p a b -> p b a").broadcast_to([P,8,LMK]),ALU.subtract)
                    step(i)
                    dve.wait_ge(ac,done)
                    for j in range(LP): i=nc.vector.tensor_reduce(out=s1[:,w,j],in_=dst[:,j].rearrange("p (b m) -> p b m",m=LMK),axis=X_AX,op=ALU.add)
                    step(i)
                    step(nc.vector.reciprocal(s1[:,w],s1[:,w]))
                    for j in range(LP): i=nc.vector.tensor_tensor(dst[:,j].rearrange("p (b m) -> p b m",m=LMK),dst[:,j].rearrange("p (b m) -> p b m",m=LMK),s1[:,w,j:j+1].rearrange("p a b -> p b a").broadcast_to([P,8,LMK]),ALU.mult)
                    step(i)
                dve.wait_ge(st,6)
                soft(B,A2,0,4)
                dve.wait_ge(st,7)
                soft(A,A1,1,5)
                dve.wait_ge(st,8)
                step(nc.vector.tensor_reduce(out=mx[:,2,:,0],in_=B[:,:,:],axis=X_AX,op=ALU.max))
                step(nc.vector.tensor_scalar(mx[:,2,:,1],mx[:,2,:,0],-1.0,None,ALU.mult))
                dve.wait_ge(ac,6)
                step(nc.vector.reciprocal(i3[:,:],mx[:,2,:,2]))
                dve.wait_ge(st,9)
                nc.vector.tensor_reduce(out=cm[:,0:1],in_=B[:,:,:],axis=mybir.AxisListType.XY,op=ALU.max)
                i=nc.vector.tensor_reduce(out=kl[:,:,0:8],in_=A2[:,:,:].rearrange("p j (b m) -> p j b m",m=LMK),axis=X_AX,op=ALU.add)
                step(i)
                step(nc.vector.tensor_reduce(out=cm[:,1:2],in_=kl[:,:,0:8],axis=mybir.AxisListType.XY,op=ALU.max))
                dve.wait_ge(st,11)
                step(nc.vector.tensor_copy(A3T[:,:,:,:],B[:,:,:].rearrange("p t (j m) -> p t j m",j=LP)))
                dve.wait_ge(st,12)
                step(nc.vector.tensor_reduce(out=m2[:,0:2],in_=A[0:1,0,0:2*P].rearrange("p (a b) -> p a b",a=2),axis=X_AX,op=ALU.max))
                step(nc.vector.tensor_tensor(m2[:,2:3],m2[:,0:1],m2[:,1:2],ALU.mult))
                step(nc.vector.reciprocal(m2[:,3:4],m2[:,2:3]))
                for h in range(2): i=nc.vector.tensor_copy(A2b[h*DH:(h+1)*DH,:,h*DH:(h+1)*DH],A2[h*DH:(h+1)*DH,:,0:LMK])
                step(i)
                dve.wait_ge(st,13)
                step(nc.vector.tensor_copy(rs[:,:],A[:,1,0:1]))
            @block.scalar
            def _(act):
                act.wait_ge(const,5); act.wait_ge(st,1)
                for h in range(2):
                    for j in range(LP):
                        i=nc.scalar.activation(qbd[h*DH:(h+1)*DH,j,:,h*DH:(h+1)*DH],A[h*DH:(h+1)*DH,j].rearrange("p (b m) -> p b m",m=LMK),ACT.Copy,scale=DH**-0.5/GROUP)
                i.then_inc(ac,1)
                act.wait_ge(st,3)
                nc.scalar.activation(qT[:,:,:],A[:,:,:],ACT.Copy,scale=DH**-0.5).then_inc(ac,1)
                act.wait_ge(st,5)
                nc.scalar.activation(v[:,:,:],A[:,:,:],ACT.Copy).then_inc(ac,1)
                act.wait_ge(dv,5)
                nc.scalar.activation(A2[:,:,:],A2[:,:,:],ACT.Exp).then_inc(ac,1)
                act.wait_ge(dv,10)
                nc.scalar.activation(A1[:,:,:],A1[:,:,:],ACT.Exp).then_inc(ac,1)
                act.wait_ge(dv,15)
                for j in range(LP): i=nc.scalar.activation(A3[:,j],B[:,j],ACT.Exp,bias=mx[:,2,j,1:2],accum_out=mx[:,2,j,2:3])
                i.then_inc(ac,1)
                act.wait_ge(st,10)
                nc.scalar.activation(A1T[:,:,:],A[:,:,:],ACT.Copy).then_inc(ac,1)
            @block.tensor
            def _(pe):
                def proj(ps,part,src):
                    for j in range(LP):
                        for k in range(2): i=nc.tensor.matmul(ps[:,j,:],wqkv[:,k,part*LI+j*P:part*LI+(j+1)*P],src[k],start=(k==0),stop=(k==1))
                    i.then_inc(st,1)
                pe.wait_ge(dv,1)
                proj(A,0,[lm[:,k,:] for k in range(2)])
                proj(B,1,[lm[:,k,:] for k in range(2)])
                tok=[HT[:,k,0,:] for k in range(2)]
                pe.wait_ge(ac,1); proj(A,0,tok)
                pe.wait_ge(dv,2); proj(B,1,tok)
                pe.wait_ge(ac,2)
                for t in range(4):
                    for k in range(2): i=nc.tensor.matmul(A[:,t,:],HT[:,k,0,t*P:(t+1)*P],wqkv[:,k,2*LI:3*LI],start=(k==0),stop=(k==1))
                i.then_inc(st,1)
                pe.wait_ge(dv,3)
                for j in range(LP):
                    for b in range(NB): i=nc.tensor.matmul(B[:,j,b*LMK:(b+1)*LMK],qbd[:,j,b],kl[:,j,b*LMK:(b+1)*LMK],start=True,stop=True)
                i.then_inc(st,1)
                pe.wait_ge(ac,3)
                for t in range(4):
                    for j in range(LP): i=nc.tensor.matmul(A[:,t,j*P:(j+1)*P],qT[:,j,t*P:(t+1)*P],klbd[:,j],start=True,stop=True)
                i.then_inc(st,1)
                pe.wait_ge(dv,5)
                for j in range(LP): i=nc.tensor.matmul(B[:,j,:],qbd[:,j,0],kT[:,j],start=True,stop=True)
                i.then_inc(st,1)
                pe.wait_ge(dv,14); pe.wait_ge(ac,6); pe.wait_ge(const,7)
                for j in range(LP): i=nc.tensor.matmul(B[:,j,:],bd[:,:],A2[:,j],start=True,stop=True)
                i.then_inc(st,1)
                for j in range(LP):
                    for t in range(4): i=nc.tensor.transpose(A[:,j,t*P:(t+1)*P],A1[:,t,j*P:(j+1)*P],ident[:,:])
                i.then_inc(st,1)
                pe.wait_ge(dv,17)
                for t in range(4):
                    for j in range(LP): i=nc.tensor.transpose(B[:,t,j*P:(j+1)*P],A3[:,j,t*P:(t+1)*P],ident[:,:])
                i.then_inc(st,1)
                pe.wait_ge(dv,18); pe.wait_ge(ac,7)
                for q in range(2): i=nc.tensor.transpose(A[0:1,0,q*P:(q+1)*P],cm[:,q:q+1],ident[:,:])
                i.then_inc(st,1)
                pe.wait_ge(dv,22)
                nc.tensor.matmul(A[:,1,0:1],one[:,:],m2[:,3:4],start=True,stop=True).then_inc(st,1)
        with ExitStack() as c2:
            sb2=lambda n,s,d=F32: c2.enter_context(nc.sbuf_tensor("pinv_"+n,s,d))
            sem2=c2.enter_context(semaphores(nc,"pinv_"))
            xt=sb2("xt",[P,LP,P]); z=sb2("z",[P,LP,P]); zt=sb2("zt",[P,LP,P]); y=sb2("y",[P,LP,P]); r=sb2("r",[P,LP,P]); t1=sb2("t1",[P,LP,P]); t2=sb2("t2",[P,LP,P]); o=sb2("o",[P,LP,T])
            ps=[c2.enter_context(nc.psum_tensor(f"pinv_ps{i}",[P,512],F32)) for i in range(4)]; po=c2.enter_context(nc.psum_tensor("pinv_po",[P,4,512],F32))
            dv,ac,st=[sem2(n) for n in ("dv","ac","st")]
            idl=ident[:,:].rearrange("p (a n) -> p a n",a=1).broadcast_to([P,LP,P])
            f=lambda a: a.rearrange("p j n -> p (j n)")
            g=lambda a: a.rearrange("p (j n) -> p j n",j=LP)
            block=c2.enter_context(nc.Block())
            @block.tensor
            def _(pe):
                def prod(dst,l,rr):
                    for j in range(LP): i=nc.tensor.matmul(dst[:,j*P:(j+1)*P],l[:,j],rr[:,j],start=True,stop=True)
                    i.then_inc(st,1)
                for j in range(LP): i=nc.tensor.transpose(ps[0][:,j*P:(j+1)*P],A2b[:,j],ident[:,:])
                i.then_inc(st,1)
                for j in range(LP):
                    for t in range(4): i=nc.tensor.matmul(ps[3][:,j*P:(j+1)*P],A3T[:,t,j],v[:,t,j*P:(j+1)*P],start=(t==0),stop=(t==3))
                i.then_inc(st,1)
                pe.wait_ge(dv,3)
                for it in range(PINV):
                    n=3+5*it
                    pe.wait_ge(dv,n); prod(ps[0],xt,z)
                    pe.wait_ge(dv,n+2); prod(ps[1],y,r)
                    pe.wait_ge(dv,n+3)
                    if it: pe.wait_ge(ac,it)
                    prod(ps[2],y,r)
                    pe.wait_ge(dv,n+4)
                    prod(ps[1],zt,r)
                    prod(ps[2],r,zt)
                pe.wait_ge(dv,3+5*PINV); pe.wait_ge(ac,PINV)
                prod(ps[0],zt,t1)
                pe.wait_ge(dv,4+5*PINV)
                for j in range(LP):
                    nc.tensor.matmul(po[:,j,:],t2[:,j],A1T[:,j],start=True,stop=False,skip_group_check=True)
                    for t in range(4):
                        a=TAPS//2 if t==0 else 0; e=WIN-TAPS//2 if t==3 else WIN
                        for h in range(2): i=nc.tensor.matmul(po[h*DH:(h+1)*DH,j,t*P-TAPS//2+a:t*P-TAPS//2+e],v[:,t,j*P+h*DH:j*P+(h+1)*DH],taps[:,2*j+h,a:e],start=False,stop=(t==3),skip_group_check=True)
                i.then_inc(st,1)
                pe.wait_ge(ac,1+PINV)
                for q in range(2):
                    for j in range(LP): i=nc.tensor.matmul(ps[q][:,:],out_w[:,j,q*P:(q+1)*P],o[:,j],start=(j==0),stop=(j==LP-1))
                i.then_inc(st,1)
            @block.vector
            def _(dve):
                c_=[0]
                def step(i):
                    c_[0]+=1; i.then_inc(dv,1); dve.wait_ge(dv,c_[0])
                dve.wait_ge(st,1)
                nc.vector.tensor_copy(f(xt),ps[0][:,:])
                nc.vector.tensor_scalar(f(z),ps[0][:,:],rs[:,0:1],None,ALU.mult)
                step(nc.vector.tensor_scalar(f(zt),f(A2b),rs[:,0:1],None,ALU.mult))
                dve.wait_ge(st,2)
                for j in range(LP): i=nc.vector.scalar_tensor_tensor(out=t1[:,j],in0=ps[3][:,j*P:(j+1)*P],scalar=i3[:,j:j+1],in1=bd[:,:],op0=ALU.mult,op1=ALU.mult)
                step(i); step(nc.vector.tensor_copy(r[:,:,:],z[:,:,:]))
                for it in range(PINV):
                    s=2+5*it
                    dve.wait_ge(st,s+1)
                    step(nc.vector.tensor_copy(f(y),ps[0][:,:]))
                    step(nc.vector.scalar_tensor_tensor(out=r[:,:,:],in0=idl,scalar=7.0,in1=y[:,:,:],op0=ALU.mult,op1=ALU.subtract))
                    dve.wait_ge(st,s+2)
                    step(nc.vector.scalar_tensor_tensor(out=r[:,:,:],in0=idl,scalar=15.0,in1=g(ps[1][:,:]),op0=ALU.mult,op1=ALU.subtract))
                    dve.wait_ge(st,s+3)
                    step(nc.vector.scalar_tensor_tensor(out=r[:,:,:],in0=idl,scalar=13.0,in1=g(ps[2][:,:]),op0=ALU.mult,op1=ALU.subtract))
                    dve.wait_ge(st,s+4)
                    step(nc.vector.tensor_scalar(f(z),ps[1][:,:],0.25,None,ALU.mult))
                dve.wait_ge(st,2+5*PINV+1)
                step(nc.vector.tensor_copy(f(t2),ps[0][:,:]))
                dve.wait_ge(st,2+5*PINV+3)
                for q in range(2): i=nc.vector.tensor_scalar(xg[:,q],ps[q][:,:],out_b[:,q:q+1],None,ALU.add)
                step(i)
            @block.scalar
            def _(act):
                for it in range(PINV):
                    act.wait_ge(st,2+5*it+5)
                    nc.scalar.activation(f(zt),ps[2][:,:],ACT.Copy,scale=0.25).then_inc(ac,1)
                act.wait_ge(st,2+5*PINV+2)
                nc.scalar.activation(o[:,:,:],po[:,:,:],ACT.Copy).then_inc(ac,1)


def adjacency_stage(nc, XT, HT, xg, rows_in, cols_in, vals_in, wq_w, wk_w, wv_w, wv_b, cols_dram):
    I32=mybir.dt.int32
    with ExitStack() as ctx:
        sb=lambda n,s,d=F32: ctx.enter_context(nc.sbuf_tensor("adj_"+n,s,d))
        sem=ctx.enter_context(semaphores(nc,"adj_"))
        ones=sb("ones",[P,P]); alpha=sb("alpha",[P,T]); wv=sb("wv",[P,2,D]); bv=sb("bv",[P,2])
        with ExitStack() as c1:
            sb1=lambda n,s,d=F32: c1.enter_context(nc.sbuf_tensor("edge_"+n,s,d))
            sem1=c1.enter_context(semaphores(nc,"edge_"))
            wq=sb1("wq",[P,2,2*DH]); wk=sb1("wk",[P,2,DH]); enc=sb1("enc",[P,2,T]); q2=sb1("q2",[P,T]); k16=sb1("k16",[P,4,2,DH],F16)
            ri=sb1("ri",[P,ECH],I32); rf=sb1("rf",[P,ECH]); va=sb1("va",[P,ECH]); ci=sb1("ci",[NGRP,CPG],I32); cf=sb1("cf",[NGRP,CPG],F16)
            io_i=sb1("io_i",[P,T],I32); iot=sb1("iot",[P,T],F16); pc_i=sb1("pc_i",[P,4],I32); pc=sb1("pc",[P,4])
            cb=sb1("cb",[P,2,PRE*CPG],F16); CT=sb1("CT",[P,PRE,4,CPG],F16); R=sb1("R",[P,PRE,EGRP,T],F16)
            raw=sb1("raw",[P,2,EGRP,DH]); kv=sb1("kv",[P,2,EGRP,DH]); kvp=sb1("kvp",[P,2,EGRP,2,DH],F16); zl=sb1("zl",[P,P],F16); zr=sb1("zr",[P,T],F16)
            pr=sb1("pr",[P,T]); st=sb1("st",[P,4])
            ps_q=c1.enter_context(nc.psum_tensor("edge_q",[P,512],F32)); ps_k=c1.enter_context(nc.psum_tensor("edge_k",[P,512],F32)); ps_g=c1.enter_context(nc.psum_tensor("edge_g",[P,2,512],F32)); ps_s=c1.enter_context(nc.psum_tensor("edge_s",[P,512],F32)); ps_a=c1.enter_context(nc.psum_tensor("edge_a",[P,512],F32))
            w_in,cols_i,rows_i,cols_out,const,enc_made,proj,khi,prep,matched,gathered,lo_kept,weighed,high,low,placed,total,products,spread,maxed,exped,alphad,dvp=[sem1(n) for n in "w_in,cols_i,rows_i,cols_out,const,enc_made,proj,khi,prep,matched,gathered,lo_kept,weighed,high,low,placed,total,products,spread,maxed,exped,alphad,dvp".split(",")]
            raw_kept=sem1("raw_kept"); onehot=sem1("onehot"); spread_in=[sem1(f"spread_in{i}") for i in range(2)]; pool_passed=sem1("pool_passed"); pe_passed=sem1("pe_passed")
            NL=NGRP//PRE
            block=c1.enter_context(nc.Block())
            @block.sync
            def _(sp):
                c1.enter_context(nc.allow_non_contiguous_dma(reason="a few small vectors"))
                sp.dma_start(ci[:,:],cols_in.rearrange("(g e) -> g e",e=CPG)).then_inc(cols_i,16)
                for h in range(2): sp.dma_start(wq[:,:,h*DH:(h+1)*DH],wq_w.rearrange("(k p) n -> p k n",p=P)).then_inc(w_in,16)
                sp.dma_start(wk[:,:,:],wk_w.rearrange("(k p) n -> p k n",p=P)).then_inc(w_in,16)
                sp.dma_start(ri[:,:],rows_in).then_inc(rows_i,16)
                sp.dma_start(va[:,:],vals_in).then_inc(rows_i,16)
                sp.dma_start(wv[:,:,:],wv_w.rearrange("(k p) n -> p k n",p=P)).then_inc(w_in,16)
                sp.dma_start(bv[:,:],wv_b.rearrange("(k p) -> p k",p=P)).then_inc(w_in,16)
                sp.wait_ge(prep,1)
                sp.dma_start(cols_dram.rearrange("(g e) -> g e",e=CPG),cf[:,:]).then_inc(cols_out,16)
                sp.wait_ge(cols_out,16)
                src=cols_dram.rearrange("(l e) -> l e",e=PRE*CPG)
                with sp.Fori(0,NL//2) as it:
                    for s in range(2):
                        sp.wait_ge(matched,it*2*PRE+s*PRE)
                        sp.dma_start(cb[:,s],src[bass.ds(it*2+s,1),:].broadcast_to([P,PRE*CPG])).then_inc(spread_in[s],16)
            @block.gpsimd
            def _(pool):
                nc.gpsimd.iota(io_i[:,:],pattern=[[1,T]],base=0,channel_multiplier=0).then_inc(const,1)
                nc.gpsimd.iota(pc_i[:,:],pattern=[[P,4]],base=0,channel_multiplier=1).then_inc(const,1)
                nc.gpsimd.memset(ones[:,:],1.0).then_inc(const,1)
                nc.gpsimd.memset(zl[:,:],0.0).then_inc(const,1)
                nc.gpsimd.memset(zr[:,:],0.0).then_inc(const,1)
                for k in range(2): i=nc.gpsimd.tensor_tensor(enc[:,k],HT[:,k,0,:],xg[:,k],ALU.add)
                i.then_inc(enc_made,1)
                with pool.Fori(0,NGRP//2) as it:
                    for s in range(2):
                        pool.wait_ge(high,it*2+s+1)
                        pool.sem_inc(pool_passed,1)
                        nc.gpsimd.tensor_tensor(kvp[:,s,:,1],kv[:,s],kvp[:,s,:,0],ALU.subtract).then_inc(low,1)
            @block.vector
            def _(dve):
                c_=[0]
                def step(i):
                    c_[0]+=1; i.then_inc(dvp,1); dve.wait_ge(dvp,c_[0])
                dve.wait_ge(cols_i,16)
                nc.vector.tensor_scalar(cf[:,:],ci[:,:],float(T-1),None,ALU.min).then_inc(prep,1)
                dve.wait_ge(rows_i,32); dve.wait_ge(const,5)
                nc.vector.tensor_copy(iot[:,:],io_i[:,:])
                nc.vector.tensor_copy(pc[:,:],pc_i[:,:])
                step(nc.vector.tensor_copy(rf[:,:],ri[:,:]))
                dve.wait_ge(khi,1)
                for t in range(4): i=nc.vector.tensor_tensor(k16[:,t,1],ps_k[:,t*DH:(t+1)*DH],k16[:,t,0],ALU.subtract)
                step(i)
                dve.sem_inc(matched,PRE)
                def match(it,j):
                    n=it*2*PRE+j; s,g_=divmod(j,PRE)
                    if g_==0: dve.wait_ge(spread_in[s],(it+1)*16)
                    dve.wait_ge(placed,n)
                    for t in range(4): i=nc.vector.tensor_scalar(CT[:,g_,t],cb[:,s,g_*CPG:(g_+1)*CPG],pc[:,t:t+1],None,ALU.is_equal)
                    i.then_inc(matched,1)
                    for c in range(EGRP): i=nc.vector.tensor_scalar(R[:,g_,c],iot[:,:],rf[:,bass.ds(n*EGRP+c,1)],None,ALU.is_equal)
                    i.then_inc(onehot,1)
                def weigh_keys(n,u):
                    dve.wait_ge(raw_kept,n+1)
                    nc.vector.tensor_tensor(raw[:,u],raw[:,u],ps_g[:,u,:].rearrange("p (c q d) -> p c q d",q=2,d=DH)[:,:,1],ALU.add).then_inc(lo_kept,1)
                    dve.wait_ge(lo_kept,n+1)
                    nc.vector.tensor_tensor(kv[:,u],raw[:,u],va[:,bass.ds(n*EGRP,EGRP)].rearrange("p (c a) -> p c a",a=1).broadcast_to([P,EGRP,DH]),ALU.mult).then_inc(weighed,1)
                with dve.Fori(0,NL//2) as it:
                    match(it,0)
                    for j in range(2*PRE):
                        if j+1<2*PRE: match(it,j+1)
                        weigh_keys(it*2*PRE+j,j%2)
                dve.wait_ge(total,1)
                nc.vector.tensor_tensor(pr[:,:],ps_s[:,:],q2[:,:],ALU.mult).then_inc(products,1)
                dve.wait_ge(spread,1)
                nc.vector.tensor_reduce(out=st[:,0:1],in_=ps_a[:,:],axis=X_AX,op=ALU.max).then_inc(maxed,1)
                dve.wait_ge(maxed,1)
                nc.vector.tensor_scalar(st[:,1:2],st[:,0:1],-(DH**-0.5),None,ALU.mult).then_inc(maxed,1)
                dve.wait_ge(exped,1)
                nc.vector.reciprocal(st[:,3:4],st[:,2:3]).then_inc(maxed,1)
                dve.wait_ge(maxed,3)
                nc.vector.tensor_scalar(alpha[:,:],alpha[:,:],st[:,3:4],None,ALU.mult).then_inc(alphad,1)
            @block.scalar
            def _(act):
                act.wait_ge(proj,2)
                nc.scalar.activation(q2[:,:],ps_q[:,:],ACT.Copy)
                nc.scalar.activation(k16[:,:,0],ps_k[:,0:4*DH].rearrange("p (t d) -> p t d",t=4),ACT.Copy).then_inc(khi,1)
                with act.Fori(0,NGRP//2) as it:
                    for s in range(2):
                        act.wait_ge(gathered,it*2+s+1)
                        act.wait_ge(weighed,it*2+s-1) if s else act.wait_ge(weighed,it*2)
                        nc.scalar.activation(raw[:,s],ps_g[:,s,:].rearrange("p (c q d) -> p c q d",q=2,d=DH)[:,:,0],ACT.Copy).then_inc(raw_kept,1)
                        act.wait_ge(weighed,it*2+s+1)
                        nc.scalar.activation(kvp[:,s,:,0],kv[:,s],ACT.Copy).then_inc(high,1)
                act.wait_ge(maxed,2)
                nc.scalar.activation(alpha[:,:],ps_a[:,:],ACT.Exp,scale=DH**-0.5,bias=st[:,1:2],accum_out=st[:,2:3]).then_inc(exped,1)
            @block.tensor
            def _(pe):
                pe.wait_ge(w_in,16*5); pe.wait_ge(enc_made,1)
                for k in range(2): i=nc.tensor.matmul(ps_q[:,:],wq[:,k],enc[:,k],start=(k==0),stop=(k==1))
                i.then_inc(proj,1)
                for t in range(4):
                    for k in range(2): i=nc.tensor.matmul(ps_k[:,t*DH:(t+1)*DH],enc[:,k,t*P:(t+1)*P],wk[:,k],start=(k==0),stop=(k==1))
                i.then_inc(proj,1)
                nc.tensor.matmul(ps_s[:,:],zl[:,:],zr[:,:],start=True,stop=False,skip_group_check=True)
                pe.wait_ge(dvp,2)
                pe.sem_inc(placed,PRE-1)
                def gather(n,s):
                    pe.wait_ge(matched,n+1+PRE)
                    if s: pe.wait_ge(weighed,n-1)
                    else: pe.wait_ge(weighed,n)
                    pe.sem_inc(pe_passed,1)
                    for c in range(EGRP):
                        for t in range(4): i=nc.tensor.matmul(ps_g[:,s%2,c*P:(c+1)*P],CT[:,s%PRE,t,c*P:(c+1)*P],k16[:,t].rearrange("p q d -> p (q d)"),start=(t==0),stop=(t==3))
                    i.then_inc(gathered,1)
                def place(n,s):
                    pe.wait_ge(low,n+1)
                    pe.wait_ge(onehot,n+1)
                    pe.sem_inc(pe_passed,1)
                    for c in range(EGRP): i=nc.tensor.matmul(ps_s[:,:],kvp[:,s%2,c].rearrange("p q d -> p (q d)"),R[:,s%PRE,c],start=False,stop=False,skip_group_check=True)
                    i.then_inc(placed,1)
                with pe.Fori(0,NL//2) as it:
                    gather(it*2*PRE,0)
                    for j in range(2*PRE):
                        if j+1<2*PRE: gather(it*2*PRE+j+1,j+1)
                        place(it*2*PRE+j,j)
                nc.tensor.matmul(ps_s[:,:],zl[:,:],zr[:,:],start=False,stop=True,skip_group_check=True).then_inc(total,1)
                pe.wait_ge(products,1)
                nc.tensor.matmul(ps_a[:,:],ones[:,:],pr[:,:],start=True,stop=True).then_inc(spread,1)
        passed=sem("pool_passed")
        value,xled,sigd,squared,diffed,moved,mixed,doubled,enced=[sem(n) for n in "value,xled,sigd,squared,diffed,moved,mixed,doubled,enced".split(",")]
        xl=sb("xl",[P,2,2,T]); sg=sb("sg",[P,2,2,T]); en=sb("en",[P,2,2,T]); df=sb("df",[P,2,2,T])
        ps_v=ctx.enter_context(nc.psum_tensor("adj_v",[P,2,2,512],F32))
        block=ctx.enter_context(nc.Block())
        @block.tensor
        def _(pe):
            with pe.Fori(0,NB//2) as it:
                for s in range(2):
                    b=it*2+s
                    pe.wait_ge(xled,b-1) if s else pe.wait_ge(xled,it*2)
                    for o in range(2):
                        for k in range(2): i=nc.tensor.matmul(ps_v[:,s,o,:],wv[:,k,o*P:(o+1)*P],HT[:,k,bass.ds(b,1),:].rearrange("p a t -> p (a t)"),start=(k==0),stop=(k==1))
                    i.then_inc(value,1)
        @block.vector
        def _(dve):
            def weigh(b,s,done):
                dve.wait_ge(value,b+1); dve.wait_ge(doubled,done)
                for o in range(2): i=nc.vector.scalar_tensor_tensor(out=xl[:,s,o],in0=ps_v[:,s,o,:],scalar=bv[:,o:o+1],in1=alpha[:,:],op0=ALU.add,op1=ALU.mult)
                i.then_inc(xled,1)
            with dve.Fori(0,NB//2) as it:
                weigh(it*2,0,it*2); weigh(it*2+1,1,it*2)
                for s in range(2):
                    b=it*2+s
                    dve.wait_ge(squared,b+1); dve.wait_ge(diffed,b+1)
                    nc.vector.tensor_tensor(df[:,s],df[:,s],sg[:,s],ALU.mult).then_inc(moved,1)
                    dve.wait_ge(mixed,b+1)
                    x_=XT[:,:,bass.ds(b,1),:].rearrange("p k a t -> p k (a t)")
                    nc.vector.scalar_tensor_tensor(out=x_,in0=df[:,s],scalar=2.0,in1=x_,op0=ALU.mult,op1=ALU.add).then_inc(doubled,1)
        @block.scalar
        def _(act):
            with act.Fori(0,NB//2) as it:
                for s in range(2):
                    b=it*2+s
                    act.wait_ge(xled,b+1)
                    act.wait_ge(moved,b-1) if s else act.wait_ge(moved,it*2)
                    nc.scalar.activation(sg[:,s],xl[:,s],ACT.Sigmoid,scale=-1.0).then_inc(sigd,1)
                    act.wait_ge(sigd,b+1)
                    nc.scalar.activation(sg[:,s],sg[:,s],ACT.Square).then_inc(squared,1)
        @block.gpsimd
        def _(pool):
            with pool.Fori(0,NB//2) as it:
                for s in range(2):
                    b=it*2+s
                    pool.wait_ge(mixed,b-1) if s else pool.wait_ge(mixed,it*2)
                    pool.sem_inc(passed,1)
                    nc.gpsimd.tensor_tensor(en[:,s],HT[:,:,bass.ds(b,1),:].rearrange("p k a t -> p k (a t)"),xg[:,:,:],ALU.add).then_inc(enced,1)
                    pool.wait_ge(enced,b+1)
                    pool.wait_ge(xled,b+1)
                    pool.wait_ge(doubled,b-1) if s else pool.wait_ge(doubled,it*2)
                    pool.sem_inc(passed,1)
                    nc.gpsimd.tensor_tensor(df[:,s],xl[:,s],en[:,s],ALU.subtract).then_inc(diffed,1)
                    pool.wait_ge(moved,b+1)
                    pool.sem_inc(passed,1)
                    nc.gpsimd.tensor_tensor(df[:,s],df[:,s],en[:,s],ALU.add).then_inc(mixed,1)


def lstm_stage(nc, XT, HT, wx, wh, bias, h0T, T=T):
    with ExitStack() as ctx:
        sb=lambda n,s,d=F32: ctx.enter_context(nc.sbuf_tensor(n,s,d))
        sem=ctx.enter_context(semaphores(nc,"lstm_"))
        banks=ctx.enter_context(nc.psum_tensor("banks",[P,2,2,2,512],F32))
        xs=sb("xs",[P,2,2,2,2,C//2,NB],F16)
        wxp=sb("wxp",[P,2,2,1024],F16); whp=sb("whp",[P,2,2,1024],F16); bp=sb("bp",[1,2,1024],F16)
        hp=sb("hp",[P,2,2,NB],F16)
        hist=sb("hist",[P,2,2*C,NB])
        cell=sb("cell",[P,2,NB])
        sig=sb("sig",[P,4,2,NB])
        t1=sb("t1",[P,2,NB]); t2=sb("t2",[P,2,NB]); tc=sb("tc",[P,2,NB])
        ones=sb("ones_row",[1,C//2*NB],F16)
        x_staged=sem("x_staged"); x_hi=sem("x_hi"); cell_cleared=sem("cell_cleared"); zeroed=sem("zeroed"); zeros=sb("zeros",[P,C//2,NB]); x_fp32=sem("x_fp32"); xf=sb("xf",[P,2,2,C//2,NB]); split=sem("split"); hi_ready=sem("hi_ready"); wsplit=sem("wsplit"); h0split=sem("h0split"); x_projected=sem("x_projected")
        ifg_ready=sem("ifg_ready"); o_ready=sem("o_ready")
        ifg_sig=sem("ifg_sig"); o_sig=sem("o_sig")
        part_ready=sem("part_ready"); cell_ready=sem("cell_ready"); tanh_ready=sem("tanh_ready"); h_ready=sem("h_ready")
        hist_saved=sem("hist_saved")
        init=sem("init")
        NIT=T//(2*C); W=C//2*NB
        block=ctx.enter_context(nc.Block())
        def gate_bank(st,par,o): return banks[:,st,o,par,0:(2 if o else 6)*W].rearrange("p (g s b) -> p g s b",g=2 if o else 6,b=NB)
        IFG=[(0,gate,u) for gate in range(3) for u in range(2)]
        O=[(1,0,u) for u in range(2)]
        def column(o,gate,u): return (2*256 if o else (0,256,768)[gate])+u*128
        @block.gpsimd
        def _(pool):
            nc.gpsimd.memset(ones[:,:],1.0).then_inc(init,1)
            nc.gpsimd.memset(zeros[:,:,:],0.0).then_inc(zeroed,1)
            pool.wait_ge(zeroed,1)
            pool.sem_inc(hist_saved,4)
            x_hi_n=[0]
            def stage(st,half,it=None):
                for par in range(2):
                    for k in range(2):
                        src=XT[:,k,:,:].rearrange("p b (s q) -> p q s b",q=2)[:,par]
                        piece=src[:,bass.ds(half,C//2),:]
                        nc.gpsimd.tensor_copy(xf[:,k,par], piece).then_inc(x_fp32,1)
                        pool.wait_ge(x_fp32, (it*8 if it is not None else 0)+x_hi_n[0]+1)
                        nc.gpsimd.tensor_tensor(xs[:,st,0,k,par], xf[:,k,par], zeros[:,:,:], ALU.add).then_inc(x_hi,1)
                        x_hi_n[0]+=1
                        pool.wait_ge(x_hi, (it*8 if it is not None else 0)+x_hi_n[0])
                        nc.gpsimd.tensor_tensor(xs[:,st,1,k,par], xf[:,k,par], xs[:,st,0,k,par], ALU.subtract).then_inc(x_staged,1)
            stage(0,0)
            with pool.Fori(0,NIT) as it:
                for st in range(2):
                    pool.wait_ge(x_projected, it*2+st+1)
                    stage(1-st, it*C+C//2 if st==0 else (it*C+C)%(T//2), it)
                    pool.wait_ge(h_ready, it*2*C+C*(st+1))
                    for u in range(2):
                        nc.gpsimd.tensor_copy(HT[:,u,:,bass.ds(it*2*C+st*C,C)].rearrange("p b t -> p t b"), hist[:,u,st*C:(st+1)*C,:]).then_inc(hist_saved,1)
        @block.tensor
        def _(pe):
            def project(st,par,tiles):
                for o,gate,u in tiles:
                    col=column(o,gate,u); out=gate_bank(st,par,o)[:,gate*2+u]
                    for part in range(2):
                        nc.tensor.matmul(out, bp[0:1,part,col:col+128], ones[0:1,:], start=(gate==0 and u==0 and part==0),stop=False,skip_group_check=True)
                    for k in range(2):
                        for wpart,xpart in ((0,0),(1,0),(0,1)):
                            last=nc.tensor.matmul(out, wxp[:,wpart,k,col:col+128], xs[:,st,xpart,k,par], start=False,stop=False,skip_group_check=True)
                return last
            pe.wait_ge(init,1)
            pe.wait_ge(wsplit,6)
            pe.wait_ge(h0split,4)
            pe.wait_ge(x_staged,4)
            for par in range(2): last=project(0,par,IFG+O)
            last.then_inc(x_projected,1)
            def recur(st,par,j,tiles,hi):
                for k in range(2):
                    for o,gate,u in tiles:
                        col=column(o,gate,u); out=gate_bank(st,par,o)[:,gate*2+u,j]
                        for wpart,hpart in (((0,0),(1,0)) if hi else ((0,1),)):
                            last=nc.tensor.matmul(out, whp[:,wpart,k,col:col+128], hp[:,k,hpart], start=False,stop=True,skip_group_check=True)
                return last
            with pe.Fori(0,NIT) as it:
                for s in range(2*C):
                    st,cs=divmod(s,C); par=cs%2; j=cs//2
                    pe.wait_ge(hi_ready, it*2*C+s)
                    recur(st,par,j,IFG,True)
                    pe.wait_ge(h_ready, it*2*C+s)
                    recur(st,par,j,IFG,False).then_inc(ifg_ready,1)
                    recur(st,par,j,O,True)
                    recur(st,par,j,O,False).then_inc(o_ready,1)
                    if cs>=8:
                        if cs==8:
                            pe.wait_ge(x_staged, it*8+4*(st+2))
                        p2,q=divmod(cs-8,4)
                        last=project(1-st,p2,(IFG+O)[2*q:2*q+2])
                        if cs==15: last.then_inc(x_projected,1)
        @block.scalar
        def _(act):
            with act.Fori(0,NIT) as it:
                for s in range(2*C):
                    st,cs=divmod(s,C); par=cs%2; j=cs//2
                    act.wait_ge(ifg_ready, it*2*C+s+1)
                    nc.scalar.activation(sig[:,0:3].rearrange("p g u b -> p (g u) b"), gate_bank(st,par,0)[:,:,j], ACT.Sigmoid).then_inc(ifg_sig,1)
                    act.wait_ge(o_ready, it*2*C+s+1)
                    nc.scalar.activation(sig[:,3], gate_bank(st,par,1)[:,:,j], ACT.Sigmoid).then_inc(o_sig,1)
                    act.wait_ge(cell_ready, it*2*C+s+1)
                    nc.scalar.activation(tc[:,:,:], cell[:,:,:], ACT.Tanh, scale=2.0).then_inc(tanh_ready,1)
        @block.vector
        def _(dve):
            for n,(src,dst) in enumerate(((wx,wxp),(wh,whp))):
                nc.vector.tensor_copy(dst[:,0],src[:,:,:]).then_inc(wsplit,1)
                dve.wait_ge(wsplit,2*n+1)
                nc.vector.tensor_tensor(dst[:,1],src[:,:,:],dst[:,0],ALU.subtract).then_inc(wsplit,1)
            nc.vector.tensor_copy(bp[0:1,0],bias[0:1,:]).then_inc(wsplit,1)
            dve.wait_ge(wsplit,5)
            nc.vector.tensor_tensor(bp[0:1,1],bias[0:1,:],bp[0:1,0],ALU.subtract).then_inc(wsplit,1)
            for k in range(2):
                nc.vector.tensor_copy(hp[:,k,0],h0T[:,k]).then_inc(h0split,1)
                dve.wait_ge(h0split,2*k+1)
                nc.vector.tensor_tensor(hp[:,k,1],h0T[:,k],hp[:,k,0],ALU.subtract).then_inc(h0split,1)
            nc.vector.memset(cell[:,:,:],0.0).then_inc(cell_cleared,1)
            dve.wait_ge(cell_cleared,1)
            with dve.Fori(0,NIT) as it:
                for s in range(2*C):
                    dve.wait_ge(ifg_sig, it*2*C+s+1)
                    nc.vector.scalar_tensor_tensor(out=t2[:,:,:],in0=sig[:,2],scalar=-0.5,in1=sig[:,0],op0=ALU.add,op1=ALU.mult).then_inc(part_ready,1)
                    dve.wait_ge(cell_ready, it*2*C+s)
                    nc.vector.tensor_tensor(t1[:,:,:],sig[:,1],cell[:,:,:],ALU.mult).then_inc(part_ready,1)
                    dve.wait_ge(part_ready, it*4*C+2*s+2)
                    nc.vector.tensor_tensor(cell[:,:,:],t1[:,:,:],t2[:,:,:],ALU.add).then_inc(cell_ready,1)
                    dve.wait_ge(o_sig, it*2*C+s+1)
                    dve.wait_ge(tanh_ready, it*2*C+s+1)
                    nc.vector.tensor_tensor(hp[:,:,0],sig[:,3],tc[:,:,:],ALU.mult).then_inc(hi_ready,1)
                    if s%C==0:
                        dve.wait_ge(hist_saved, it*4+2*(s//C)+2)
                    nc.vector.tensor_tensor(hist[:,:,s],sig[:,3],tc[:,:,:],ALU.mult).then_inc(split,1)
                    dve.wait_ge(split,it*2*C+s+1)
                    nc.vector.tensor_tensor(hp[:,:,1],hist[:,:,s],hp[:,:,0],ALU.subtract).then_inc(h_ready,1)


def kv_tiles():
    out=[];col=0
    for t in range((KV+P-1)//P):
        q0=max(0,P*t-PM); out.append((min(P,KV-P*t),q0,col)); col+=T-q0
    return out,col


class Core: pass


def attention_core(nc, XT, HT, c_):
    NP_,BPI,TILES,PCOLS,PM=c_.pairs,c_.batch_per_turn,c_.tiles,c_.pcols,c_.pm
    W_=NP_*P
    S=NP_*BPI
    def value_jobs(s): return [s+2]
    def jobs_before(it,s): return it*S+s+2
    def outputs_before(it,s): return 2*(it*BPI+(s-1)//NP_) if s>0 else 0
    def slots(run,eng):
        for s in (-2,-1,0): run(0,s)
        with eng.Fori(0,NB//BPI) as it:
            for s in range(1,S+1): run(it,s)
    def width(qt): return min(T,P*qt+P+PM) if c_.rope else T
    with ExitStack() as ctx:
        sb=lambda n,s,d=F32: ctx.enter_context(nc.sbuf_tensor(c_.name+"_"+n,s,d))
        sem=ctx.enter_context(semaphores(nc,c_.name+"_"))
        HB=c_.h_buffers; VB=c_.v_buffers
        hT=sb("hT",[P,HB,2,2,PM+T],F16)
        V=sb("V",[P,VB,len(TILES),NP_,3,DH])
        QK=sb("QK",[P,4,2,2,PM+T],F16)
        ab=sb("ab",[P,2,T]); rot=ab[:,0]; PT=sb("PT",[P,2,PCOLS]); ao=sb("ao",[P,NP_,T])
        mx=sb("mx",[P,2,5]); mparts=sb("mparts",[P,2,4,2,2],BF16)
        mT=sb("mT",[P,2,T],BF16); sums=sb("sums",[P,T]); summed_up=sem("summed_up")
        st_ps=ctx.enter_context(nc.psum_tensor(c_.name+"_stp",[P,2,512],F32)); s_ps=ctx.enter_context(nc.psum_tensor(c_.name+"_sp",[P,2,512],F32))
        acc=ctx.enter_context(nc.psum_tensor(c_.name+"_acc",[P,2,512],F32)); pj=ctx.enter_context(nc.psum_tensor(c_.name+"_proj",[P,2,512],F32))
        mtp=s_ps[:,0,:].bitcast(BF16)
        h_hi,h_ready,v_done,v_kept,pm_kept,ones_set,proj,evac,summed,hi,lo,s_done,maxed,m_ready,m_turned,m_copied,st_done,exped,masked,pv_done,recips,normed,o_done,added,mstep,pmcopied=[sem(n) for n in "h_hi,h_ready,v_done,v_kept,pm_kept,ones_set,proj,evac,summed,hi,lo,s_done,maxed,m_ready,m_turned,m_copied,st_done,exped,masked,pv_done,recips,normed,o_done,added,mstep,pmcopied".split(",")]
        gated=sem("gated"); pe_passed=sem("pe_passed"); pool_passed=sem("pool_passed"); dve_passed=sem("dve_passed")
        NT=4
        def sliced(X,k,it): return X[:,k,bass.ds(it,1),:].rearrange("p a t -> p (a t)")
        block=ctx.enter_context(nc.Block())
        def batch(it,n): return (it*BPI+n//NP_)%NB
        def h_of(n): return hT[:,(n//NP_)%HB]
        def v_of(n): return V[:,(n//NP_)%VB]
        v_zero=sem("v_zero")
        @block.tensor
        def _(pe):
            def project(it,j):
                n,what=divmod(j,2)
                pe.wait_ge(evac, it*2*S+j)
                if what==0:
                    pe.wait_ge(added, outputs_before(it,n-2))
                    pe.wait_ge(v_kept, jobs_before(it,n-2))
                if n%NP_==0 and what==0:
                    pe.wait_ge(h_ready, 2*(it*BPI+n//NP_)+2)
                    if not c_.rope: pe.wait_ge(c_.w_ready, it*BPI+n//NP_+1)
                m=n%NP_
                for b_,col in (((0,what*W_+m*P),(1,(3+what)*W_+m*P)) if c_.rope else ((0,what*W_+m*P),)):
                    i=0
                    for k in range(2):
                        for wpart,xpart in ((0,0),(1,0),(0,1)):
                            last=nc.tensor.matmul(pj[:,b_,:],c_.w_of(n)[:,wpart,k,col:col+P],h_of(n)[:,xpart,k,PM:PM+T],start=(i==0),stop=(i==5)); i+=1
                last.then_inc(proj,1)
            def scores(it,n,qt):
                if qt==0:
                    pe.wait_ge(lo, it*2*S+2*n+2)
                    if n: pe.wait_ge(m_copied, it*S+n)
                pe.wait_ge(maxed, it*S*4+n*4+qt)
                q=QK[:,n%4,0]; k_=QK[:,n%4,1]
                jobs=[(qt,0,width(qt),0)]
                if qt==2 and PM: jobs.append((3,T,PM+T,2*P+P+PM))
                for qq,c0,c1,at in jobs:
                    for h in range(2):
                        r=slice(h*DH,(h+1)*DH)
                        last=nc.tensor.matmul(s_ps[:,h,at:at+c1-c0],q[r,0,qq*P:(qq+1)*P],k_[r,0,c0:c1],start=True,stop=True,skip_group_check=True)
                last.then_inc(s_done,1)
            def turn_max(it,n):
                pe.wait_ge(m_ready, it*S+n+1)
                pe.sem_inc(pe_passed,1)
                for qt in range(4):
                    for h in range(2):
                        last=nc.tensor.transpose(mtp[h*DH:h*DH+2,qt*P:(qt+1)*P],mparts[:,n%2,qt,h],c_.identb[:,:])
                last.then_inc(m_turned,1)
            def scores_T(it,n,t):
                if t==0: pe.wait_ge(m_copied, it*S+n+1)
                pe.wait_ge(exped, it*S*NT+n*NT+t)
                pe.sem_inc(pe_passed,1)
                q=QK[:,n%4,0]; k_=QK[:,n%4,1]
                for tt in ([t,t+1] if t==NT-1 and PM else [t]):
                    rows,q0,_=TILES[tt]; at=0 if tt==t else T-TILES[t][1]
                    for h in range(2):
                        r=slice(h*DH,(h+1)*DH)
                        nc.tensor.matmul(st_ps[0:rows,h,at:at+T-q0],c_.ones[r,0:rows],mT[r,n%2,q0:T],start=(tt==t),stop=False,skip_group_check=True)
                    for i,(qpart,kpart) in enumerate(((0,0),(1,0),(0,1))):
                        for h in range(2):
                            r=slice(h*DH,(h+1)*DH)
                            last=nc.tensor.matmul(st_ps[0:rows,h,at:at+T-q0],k_[r,kpart,tt*P:tt*P+rows],q[r,qpart,q0:T],start=False,stop=(i==2),skip_group_check=True)
                last.then_inc(st_done,1)
            def values(it,n,t):
                pe.wait_ge(masked if c_.rope else exped, it*S*NT+n*NT+t+1)
                if t==0:
                    pe.wait_ge(normed, it*S+n)
                    pe.wait_ge(v_kept, it*S+n+1)
                for tt in ([t,t+1] if t==NT-1 and PM else [t]):
                    rows,q0,col=TILES[tt]
                    for h in range(2):
                        last=nc.tensor.matmul(acc[:,h,q0:T],v_of(n)[0:rows,tt,n%NP_,h:h+2].rearrange("p a d -> p (a d)"),PT[0:rows,h,col:col+T-q0],start=(tt==0),stop=(tt==len(TILES)-1),skip_group_check=True)
                if t==NT-1: last.then_inc(pv_done,1)
            pe.wait_ge(ones_set,4)
            def project_values(it,n):
                pe.wait_ge(v_kept, it*S+n)
                col=2*W_+(n%NP_)*P
                for tt,(rows,_,_) in enumerate(TILES):
                    c=0
                    for k in range(2):
                        for wpart,xpart in ((0,0),(1,0),(0,1)):
                            last=nc.tensor.matmul(pj[0:rows,tt//4,(tt%4)*P:(tt%4+1)*P],h_of(n)[:,xpart,k,tt*P:tt*P+rows],c_.w_of(n)[:,wpart,k,col:col+P],start=(c==0),stop=(c==5)); c+=1
                last.then_inc(v_done,1)
            def outputs(it,n):
                pe.wait_ge(normed if c_.rope else gated,it*S+n+1)
                pe.wait_ge(evac,it*2*S+2*(n+3)+2)
                pe.wait_ge(v_kept,jobs_before(it,n+2))
                for m in range(2):
                    for q in range(NP_):
                        last=nc.tensor.matmul(pj[:,m,:],c_.wo[:,q,m*P:(m+1)*P],ao[:,q,:],start=(q==0),stop=(q==NP_-1))
                    last.then_inc(o_done,1)
            def slot(it,s):
                project(it,2*(s+2))
                if s>=0: turn_max(it,s); scores_T(it,s,0)
                if s>=-1: scores(it,s+1,0)
                project(it,2*(s+2)+1)
                for t in range(1,4):
                    if s>=0: scores_T(it,s,t); values(it,s,t-1)
                    if s>=-1: scores(it,s+1,t)
                    if t==1:
                        if value_jobs(s): pe.wait_ge(evac,it*2*S+2*(s+2)+2)
                        for n in value_jobs(s): project_values(it,n)
                if s>=0: values(it,s,3)
                if s>0 and s%NP_==0: outputs(it,s-1)
            slots(slot,pe)
        @block.vector
        def _(dve):
            nc.vector.memset(V[:,:,:,:,1,:],1.0).then_inc(ones_set,1)
            nc.vector.memset(hT[:,:,:,:,0:max(PM,1)],0.0).then_inc(ones_set,1)
            nc.vector.memset(mx[:,:,:],0.0).then_inc(ones_set,1)
            nc.vector.memset(mT[:,:,:],0.0).then_inc(ones_set,1)
            dve.wait_ge(ones_set,4)
            def rotate(it,j):
                dve.wait_ge(proj,it*2*S+j+1)
                if c_.rope: dve.wait_ge(lo,it*2*S+j)
                if c_.rope:
                    for q in range(2):
                        i=nc.vector.tensor_tensor(ab[:,q],pj[:,q,:],c_.tab[:,q],ALU.mult)
                    i.then_inc(evac,1)
                else:
                    n,what=divmod(j,2)
                    dve.wait_ge(hi,it*2*S+j)
                    dve.wait_ge(lo,it*2*S+j)
                    nc.vector.tensor_scalar(rot[:,:],pj[:,0,:],c_.bias(batch(it,n),what,n%NP_),c_.gate(batch(it,n),n%NP_),ALU.add,ALU.mult).then_inc(evac,1)
            def maxima(it,n,qt):
                dve.wait_ge(s_done,it*S*4+n*4+qt+1)
                if qt==0: dve.wait_ge(mstep, (it*S+n)*4)
                dve.sem_inc(dve_passed,1)
                w_=width(qt); off=(3-qt)*P if c_.rope else 0
                jobs=[(qt,0,w_,off)]
                if qt==2 and PM: jobs.append((4,w_,w_+PM,T-w_))
                for h in range(2):
                    for at,c0,c1,mo in jobs:
                        i=nc.vector.tensor_tensor_reduce(out=s_ps[:,h,c0:c1],in0=s_ps[:,h,c0:c1],in1=c_.mask[:,mo+c0:mo+c1],scale=1.0,scalar=-3e38,op0=ALU.add,op1=ALU.max,accum_out=mx[:,h,at:at+1])
                i.then_inc(maxed,1)
                if qt==3:
                    base=(it*S+n)*4
                    dve.wait_ge(maxed,it*S*4+n*4+4)
                    nc.vector.tensor_tensor(mx[:,:,3:4],mx[:,:,3:4],mx[:,:,4:5],ALU.max).then_inc(mstep,1)
                    dve.wait_ge(mstep,base+1)
                    if n: dve.wait_ge(m_turned, it*S+n-1)
                    hi_=mparts[:,n%2,:,:,0].rearrange("p q h -> p h q"); lo_=mparts[:,n%2,:,:,1].rearrange("p q h -> p h q")
                    nc.vector.tensor_scalar(hi_,mx[:,:,0:4],-1.0,None,ALU.mult).then_inc(mstep,1)
                    dve.wait_ge(mstep,base+2)
                    nc.vector.scalar_tensor_tensor(out=lo_,in0=mx[:,:,0:4],scalar=-1.0,in1=hi_,op0=ALU.mult,op1=ALU.subtract).then_inc(mstep,1)
                    dve.wait_ge(mstep,base+3)
                    nc.vector.tensor_copy(mx[:,:,4:5],mx[:,:,0:1]).then_inc(mstep,1)
                    dve.wait_ge(mstep,base+4)
                    dve.sem_inc(m_ready,1)
            def normalise(it,n):
                dve.wait_ge(pv_done,it*S+n+1)
                if n%NP_==0: dve.wait_ge(o_done,2*(it*BPI+n//NP_))
                dve.wait_ge(summed_up,it*S+n+1)
                nc.vector.reciprocal(sums[:,:],sums[:,:]).then_inc(recips,1)
                dve.wait_ge(recips,it*S+n+1)
                for h in range(2):
                    o=slice(h*DH,(h+1)*DH)
                    i=nc.vector.tensor_tensor(ao[o,n%NP_,:],acc[o,h,:],sums[o,:],ALU.mult)
                i.then_inc(normed,1)
                if not c_.rope:
                    dve.wait_ge(normed,it*S+n+1)
                    nc.vector.tensor_scalar(ao[:,n%NP_,:],ao[:,n%NP_,:],c_.bias(batch(it,n),2,n%NP_),c_.gate(batch(it,n),n%NP_),ALU.add,ALU.mult).then_inc(gated,1)
            def add_outputs(it,n):
                b=it*BPI+n//NP_
                for m in range(2):
                    dve.wait_ge(o_done,2*b+m+1)
                    if c_.rope: nc.vector.tensor_tensor(sliced(XT,m,b),sliced(XT,m,b),pj[:,m,:],ALU.add).then_inc(added,1)
                    else: nc.vector.scalar_tensor_tensor(out=sliced(XT,m,b),in0=pj[:,m,:],scalar=c_.bo[:,m:m+1],in1=sliced(XT,m,b),op0=ALU.add,op1=ALU.add).then_inc(added,1)
            def slot(it,s):
                rotate(it,2*(s+2))
                if s>=1: normalise(it,s-1)
                if s>=-1: maxima(it,s+1,0)
                rotate(it,2*(s+2)+1)
                if s>=-1:
                    for t in range(1,4): maxima(it,s+1,t)
                if s>0 and s%NP_==0: add_outputs(it,s-1)
            slots(slot,dve)
        if not c_.rope: c_.select(nc,block,ctx,hi)
        @block.scalar
        def _(act):
            def high(it,j):
                n,what=divmod(j,2)
                if what and PM: nc.scalar.activation(QK[:,n%4,1,:,0:PM],c_.pmk[:,n%NP_],ACT.Copy).then_inc(pmcopied,1)
                act.wait_ge(summed if c_.rope else evac,it*2*S+j+1)
                dst=QK[:,n%4,1,0,PM:PM+T] if what else QK[:,n%4,0,0,0:T]
                nc.scalar.activation(dst,rot[:,:],ACT.Copy).then_inc(hi,1)
            def exps(it,n,t):
                act.wait_ge(st_done,it*S*NT+n*NT+t+1)
                if t==0: act.wait_ge(pv_done,it*S+n)
                rows,q0,col=TILES[t]; w_=T-q0
                i=nc.scalar.activation(PT[0:rows,:,col:col+w_],st_ps[0:rows,:,0:w_],ACT.Exp,scale=DH**-0.5)
                if t==NT-1 and PM:
                    r2,q2,c2=TILES[NT]
                    i=nc.scalar.activation(PT[0:r2,:,c2:c2+T-q2],st_ps[0:r2,:,w_:w_+T-q2],ACT.Exp,scale=DH**-0.5)
                i.then_inc(exped,1)
            def inverse_sum(it,n):
                act.wait_ge(pv_done,it*S+n+1)
                act.wait_ge(normed,it*S+n)
                for h in range(2):
                    o,s_=slice(h*DH,(h+1)*DH),slice((1-h)*DH,(2-h)*DH)
                    i=nc.scalar.activation(sums[o,:],acc[s_,h,:],ACT.Copy)
                i.then_inc(summed_up,1)
            def keep_max(it,n):
                act.wait_ge(m_turned,it*S+n+1)
                for h in range(2):
                    r=slice(h*DH,h*DH+2)
                    i=nc.scalar.activation(mT[r,n%2,:],mtp[r,0:T],ACT.Copy)
                i.then_inc(m_copied,1)
            act.wait_ge(ones_set,4)
            def high_tokens(it,n):
                for k in range(2):
                    nc.scalar.activation(h_of(n)[:,0,k,PM:PM+T],sliced(HT,k,batch(it,n)),ACT.Copy).then_inc(h_hi,1)
                if not c_.rope: c_.high_weights(act,it*BPI+n//NP_,n)
            def keep_values(it,n):
                act.wait_ge(v_done,it*S+n+1)
                v=v_of(n)[:,:,n%NP_]
                for tt,(rows,_,_) in enumerate(TILES):
                    if tt in (1,2,3): continue
                    last=4 if tt==0 else tt+1
                    i=nc.scalar.activation(v[0:rows,tt:last,0:3:2,:],pj[0:rows,tt//4,0:(last-tt)*P].rearrange("p (t h d) -> p t h d",h=2,d=DH),ACT.Copy)
                if PM:
                    i.then_inc(v_zero,1)
                    act.wait_ge(v_zero,it*S+n+1)
                    i=nc.scalar.activation(v[0:PM,0,0:3:2,:],c_.pmv[:,n%NP_],ACT.Copy)
                i.then_inc(v_kept,1)
            def slot(it,s):
                if s>=1: inverse_sum(it,s-1)
                if s>=0: keep_max(it,s)
                high(it,2*(s+2))
                if s>=0: exps(it,s,0)
                high(it,2*(s+2)+1)
                for t in range(1,4):
                    if s>=0: exps(it,s,t)
                    if t==1:
                        for n in value_jobs(s): keep_values(it,n)
                if (s+3)%NP_==0:
                    act.wait_ge(proj,it*2*S+2*(s+3))
                    act.wait_ge(v_done,jobs_before(it,s+1))
                    high_tokens(it,s+3)
            high_tokens(0,0)
            slots(slot,act)
        @block.gpsimd
        def _(pool):
            def sum_low(it,j):
                n,what=divmod(j,2)
                if c_.rope:
                    pool.wait_ge(evac,it*2*S+j+1)
                    nc.gpsimd.tensor_tensor(rot[:,:],ab[:,0],ab[:,1],ALU.add).then_inc(summed,1)
                pool.wait_ge(hi,it*2*S+j+1)
                dst=QK[:,n%4,what,:,PM:PM+T] if what else QK[:,n%4,0,:,0:T]
                nc.gpsimd.tensor_tensor(dst[:,1],rot[:,:],dst[:,0],ALU.subtract).then_inc(lo,1)
            def hide(it,n,t):
                pool.wait_ge(exped,it*S*NT+n*NT+t+1)
                pool.sem_inc(pool_passed,1)
                rows,q0,col=TILES[t]; c=P-PM if t==0 else P
                v=PT[0:rows,:,col:col+c]
                i=nc.gpsimd.affine_select(out=v,in_=v,compare_op=ALU.is_ge,fill=0.0,base=PM if t==0 else 0,pattern=[[0,2],[1,c]],channel_multiplier=-1)
                if t==NT-1:
                    r2,q2,c2=TILES[NT]
                    v=PT[0:r2,:,c2:c2+T-q2]
                    i=nc.gpsimd.affine_select(out=v,in_=v,compare_op=ALU.is_ge,fill=0.0,base=0,pattern=[[0,2],[1,T-q2]],channel_multiplier=-1)
                i.then_inc(masked,1)
            def low_tokens(it,n):
                for k in range(2):
                    pool.wait_ge(h_hi,2*(it*BPI+n//NP_)+k+1)
                    nc.gpsimd.tensor_tensor(h_of(n)[:,1,k,PM:PM+T],sliced(HT,k,batch(it,n)),h_of(n)[:,0,k,PM:PM+T],ALU.subtract).then_inc(h_ready,1)
                if not c_.rope: c_.low_weights(pool,it*BPI+n//NP_,n)
            def slot(it,s):
                sum_low(it,2*(s+2))
                if s>=0 and c_.rope: hide(it,s,0)
                sum_low(it,2*(s+2)+1)
                if s>=0 and c_.rope:
                    for t in range(1,4): hide(it,s,t)
                if (s+3)%NP_==0: low_tokens(it,s+3)
            low_tokens(0,0)
            slots(slot,pool)


def attention_stage(nc, XT, HT, w_qkvT, w_outT, pmT, pmV, rope, ident):
    TILES,PCOLS=kv_tiles()
    with ExitStack() as ctx:
        sb=lambda n,s,d=F32: ctx.enter_context(nc.sbuf_tensor("att_"+n,s,d))
        sem=ctx.enter_context(semaphores(nc,"att_"))
        w=sb("w",[P,2,2,5*INNER_],F16)
        wo=sb("wo",[P,PAIRS,D]); tab=sb("rope",[P,2,T]); pmk=sb("pmk",[P,PAIRS,2,PM],F16); pmv=sb("pmv",[PM,PAIRS,2,DH])
        mask=sb("mask",[P,KV]); selh=sb("selh",[P,P],BF16); identb=sb("identb",[P,P],BF16)
        with ExitStack() as c1:
            st=c1.enter_context(nc.sbuf_tensor("attw_st",[P,2,2,512],F32)); pk32=c1.enter_context(nc.sbuf_tensor("attw_pk",[P,PAIRS,PM],F32))
            sem1=c1.enter_context(semaphores(nc,"attw_"))
            ld=[sem1(f"chunk_loaded{i}") for i in range(2)]; ld2=sem1("rest_loaded"); ldk=sem1("memory_keys_loaded"); hi=sem1("hi"); lo=sem1("lo"); swapped=sem1("swapped"); g=sem1("masks"); pmh=sem1("pmh"); pml=sem1("pml")
            NCH=3*INNER_//512
            block=c1.enter_context(nc.Block())
            @block.sync
            def _(sp):
                for c in range(NCH):
                    if c>=2: sp.wait_ge(lo,c-1)
                    sp.dma_start(st[:,c%2],w_qkvT[:,c*512:(c+1)*512].rearrange("(k p) n -> p k n",p=P)).then_inc(ld[c%2],16)
                    if c==0: sp.dma_start(pk32[:,:,:],pmT).then_inc(ldk,16)
                    if c==1:
                        sp.dma_start(wo[:,:,:],w_outT.rearrange("(a p) n -> p a n",p=P)).then_inc(ld2,16)
                        sp.dma_start(tab[:,:,:],rope).then_inc(ld2,16)
                        sp.dma_start(pmv[:,:,:,:],pmV).then_inc(ld2,16)
                sp.wait_ge(ld2,48)
            @block.scalar
            def _(act):
                for c in range(NCH):
                    act.wait_ge(ld[c%2],16*(c//2+1))
                    nc.scalar.activation(w[:,0,:,c*512:(c+1)*512],st[:,c%2],ACT.Copy).then_inc(hi,1)
            @block.vector
            def _(dve):
                dve.wait_ge(ldk,16)
                nc.vector.tensor_copy(pmk[:,:,0],pk32[:,:,:]).then_inc(pmh,1)
                dve.wait_ge(pmh,1)
                nc.vector.tensor_tensor(pmk[:,:,1],pk32[:,:,:],pmk[:,:,0],ALU.subtract).then_inc(pmh,1)
                nc.vector.tensor_copy(identb[:,:],ident[:,:]).then_inc(pmh,1)
                for c in range(NCH):
                    dve.wait_ge(hi,c+1)
                    nc.vector.tensor_tensor(w[:,1,:,c*512:(c+1)*512],st[:,c%2],w[:,0,:,c*512:(c+1)*512],ALU.subtract).then_inc(lo,1)
                    if c<2*INNER_//512:
                        dve.wait_ge(lo,c+1)
                        for part in range(2):
                            for k in range(2):
                                src=w[:,part,k,c*512:(c+1)*512].rearrange("p (i two) -> p i two",two=2); dst=w[:,part,k,3*INNER_+c*512:3*INNER_+(c+1)*512].rearrange("p (i two) -> p i two",two=2)
                                for q in range(2): nc.vector.tensor_copy(dst[:,:,q],src[:,:,1-q]).then_inc(swapped,1)
            @block.gpsimd
            def _(pool):
                n=[0]
                def step(i):
                    n[0]+=1; i.then_inc(g,1); pool.wait_ge(g,n[0])
                step(nc.gpsimd.memset(mask[:,:],0.0))
                step(nc.gpsimd.affine_select(out=mask[:,:],in_=mask[:,:],compare_op=ALU.is_ge,fill=MASKED,base=T-P+PM,pattern=[[-1,KV]],channel_multiplier=1))
                step(nc.gpsimd.memset(selh[:,:],1.0))
        c=Core(); c.pairs=PAIRS; c.tiles,c.pcols=TILES,PCOLS; c.rope=True; c.pm=PM; c.w=w; c.wo=wo; c.tab=tab; c.pmk=pmk; c.pmv=pmv; c.mask=mask; c.ones=selh; c.identb=identb; c.name='att'
        c.batch_per_turn=1; c.h_buffers=1; c.v_buffers=1; c.w_of=lambda n: w
        attention_core(nc,XT,HT,c)


def rope_table():
    inv=np.float32(1.0)/np.power(np.float32(10000.0),np.arange(0,DH,2,dtype=np.float32)/np.float32(DH)).astype(np.float32)
    f=(np.arange(T,dtype=np.float32)[:,None]*inv[None,:]).astype(np.float32)
    f=np.repeat(f,2,axis=-1).T
    sign=np.where(np.arange(DH)%2==0,-1,1).astype(np.float32)[:,None]
    one=np.stack([np.cos(f),np.sin(f)*sign],1).astype(np.float32)
    return np.ascontiguousarray(np.concatenate([one,one],0))


def ffn0_stage(nc, XT, HT, Wq,bq,Wk,bk,Wv,bv,Wr,br,Wo,bo, ident, g_dram, i_dram, prefetch, prefetched):
    with ExitStack() as ctx:
        sb=lambda n,s,d=F32: ctx.enter_context(nc.sbuf_tensor("sel_"+n,s,d))
        I32=mybir.dt.int32
        NP0=K0//2
        gate=sb("gate",[P,NB,NP0]); idx=sb("idx",[1,NB*K0],I32); bias=sb("bias",[P,NB,3,NP0]); wo=sb("wo",[P,NP0,D]); bo_s=sb("bo",[P,2])
        identb=sb("identb",[P,P],BF16); ones=sb("ones",[P,P],BF16); mask=sb("zeros",[P,T])
        with ExitStack() as c1:
            sb1=lambda n,s,d=F32: c1.enter_context(nc.sbuf_tensor("pick_"+n,s,d))
            sem=c1.enter_context(semaphores(nc,"pick_"))
            wr=sb1("wr",[P,2,H0]); brs=sb1("br",[1,H0]); one=sb1("one",[1,NB]); hm=sb1("hm",[P,2,NB]); lg=sb1("lg",[NB,H0]); heads_i=sb1("heads_i",[P,NB*K0,H0],I32); heads=sb1("heads",[P,NB*K0,H0]); idb=sb1("idb",[P,NB*K0],I32); idf=sb1("idf",[P,NB*K0]); is_head=sb1("is_head",[P,NB*K0,H0]); term=sb1("term",[P,3,NB*K0,H0]); bt=sb1("bt",[P,3,H0]); sc=sb1("sc",[NB,8]); dist=sb1("dist",[NB,H0]); top=sb1("top",[NB,8]); ti=sb1("ti",[NB,8],U32); e4=sb1("e4",[NB,K0]); g=sb1("g",[NB,K0])
            pl=c1.enter_context(nc.psum_tensor("pick_l",[P,512],F32))
            ld,ldb,ids,mean,lgd,dv,ex,den,wr_out,picked,bl,e0s,all_biases,spread=[sem(n) for n in "ld,ldb,ids,mean,lgd,dv,ex,den,wr_out,picked,bl,e0s,all_biases,spread".split(",")]
            block=c1.enter_context(nc.Block())
            @block.sync
            def _(sp):
                strided=c1.enter_context(nc.allow_non_contiguous_dma(reason="a few small vectors"))
                sp.dma_start(wr[:,:,:],Wr.rearrange("(k p) n -> p k n",p=P)).then_inc(ld,16)
                sp.dma_start(brs[:,:],br.rearrange("(a n) -> a n",a=1)).then_inc(ld,16)
                sp.dma_start(wo[:,:,:],Wo.rearrange("(a p) n -> p a n",p=P)).then_inc(ldb,16)
                sp.dma_start(bo_s[:,:],bo.rearrange("(k p) -> p k",p=P)).then_inc(ldb,16)
                for q,src in enumerate((bq,bk,bv)):
                    for h in range(2): sp.dma_start(bt[h*DH:(h+1)*DH,q],src.rearrange("(n d) -> d n",d=DH)).then_inc(all_biases,16)
                sp.wait_ge(dv,8)
                sp.dma_start(i_dram,ti[:,0:K0].bitcast(I32)).then_inc(wr_out,16)
                sp.wait_ge(dv,12)
                sp.dma_start(g_dram,g[:,:]).then_inc(wr_out,16)
                sp.wait_ge(wr_out,32)
                sp.dma_start(idx[:,:],i_dram.rearrange("(a b) k -> a (b k)",a=1)).then_inc(picked,16)
                for h in range(2):
                    sp.dma_start(gate[h*DH:(h+1)*DH,:,:],g_dram.rearrange("b (n h) -> h b n",h=2)[h:h+1].broadcast_to([DH,NB,NP0])).then_inc(bl,16)
                sp.dma_start(idb[:,:],i_dram.rearrange("(a b) k -> a (b k)",a=1).broadcast_to([P,NB*K0])).then_inc(spread,16)
                sp.wait_ge(picked,16); sp.wait_ge(bl,32)
                sp.wait_ge(ldb,32)
                for dst,src in prefetch: sp.dma_start(dst,src).then_inc(prefetched,16)
            @block.gpsimd
            def _(pool):
                nc.gpsimd.memset(one[:,:],1.0).then_inc(ids,1)
                nc.gpsimd.memset(ones[:,:],1.0).then_inc(ids,1)
                nc.gpsimd.memset(mask[:,:],0.0).then_inc(ids,1)
                nc.gpsimd.iota(heads_i[:,:,:],pattern=[[0,NB*K0],[1,H0]],base=0,channel_multiplier=0).then_inc(ids,1)
            @block.tensor
            def _(pe):
                pe.wait_ge(ld,32); pe.wait_ge(ids,1); pe.wait_ge(mean,2)
                for k in range(2): nc.tensor.matmul(pl[0:NB,0:H0],hm[:,k,:],wr[:,k,:],start=(k==0),stop=False)
                nc.tensor.matmul(pl[0:NB,0:H0],one[:,:],brs[:,:],start=False,stop=True).then_inc(lgd,1)
            @block.scalar
            def _(act):
                act.wait_ge(dv,4)
                nc.scalar.activation(dist[:,:],lg[:,:],ACT.Exp,bias=sc[:,0:1],accum_out=sc[:,1:2]).then_inc(ex,1)
                act.wait_ge(dv,9)
                nc.scalar.activation(e4[:,:],top[:,0:K0],ACT.Exp,bias=sc[:,2:3],accum_out=sc[:,3:4]).then_inc(ex,1)
                nc.scalar.activation(sc[:,4:5],sc[:,2:3],ACT.Exp).then_inc(ex,1)
            @block.vector
            def _(dve):
                n=[0]
                def step(i):
                    n[0]+=1; i.then_inc(dv,1); dve.wait_ge(dv,n[0])
                step(nc.vector.tensor_copy(identb[:,:],ident[:,:]))
                nc.vector.tensor_reduce(out=hm[:,:,:],in_=HT[:,:,:,:],axis=mybir.AxisListType.X,op=ALU.add).then_inc(mean,1)
                dve.wait_ge(mean,1)
                nc.vector.tensor_scalar(hm[:,:,:],hm[:,:,:],1.0/T,None,ALU.mult).then_inc(mean,1)
                dve.wait_ge(lgd,1)
                step(nc.vector.tensor_copy(lg[:,:],pl[0:NB,0:H0]))
                step(nc.vector.reduce_max(sc[:,5:6],lg[:,:],axis=mybir.AxisListType.X))
                step(nc.vector.tensor_scalar(sc[:,0:1],sc[:,5:6],-1.0,None,ALU.mult))
                dve.wait_ge(ex,1)
                step(nc.vector.reciprocal(sc[:,6:7],sc[:,1:2]))
                step(nc.vector.tensor_scalar(dist[:,:],dist[:,:],sc[:,6:7],None,ALU.mult))
                step(nc.vector.max(top[:,:],dist[:,:]))
                step(nc.vector.max_index(ti[:,:],top[:,:],dist[:,:]))
                step(nc.vector.tensor_scalar(sc[:,2:3],top[:,0:1],-1.0,None,ALU.mult))
                dve.wait_ge(ex,3)
                step(nc.vector.scalar_tensor_tensor(out=sc[:,7:8],in0=sc[:,4:5],scalar=float(H0-K0),in1=sc[:,3:4],op0=ALU.mult,op1=ALU.add))
                step(nc.vector.reciprocal(sc[:,6:7],sc[:,7:8]))
                step(nc.vector.tensor_scalar(g[:,:],e4[:,:],sc[:,6:7],None,ALU.mult))
                dve.wait_ge(ids,4); dve.wait_ge(all_biases,16*6); dve.wait_ge(spread,16)
                nc.vector.tensor_copy(heads[:,:,:],heads_i[:,:,:])
                step(nc.vector.tensor_copy(idf[:,:],idb[:,:]))
                step(nc.vector.tensor_tensor(is_head[:,:,:],heads[:,:,:],idf[:,:].rearrange("p (a b) -> p a b",b=1).broadcast_to([P,NB*K0,H0]),ALU.is_equal))
                for q in range(3): i=nc.vector.tensor_tensor(term[:,q],is_head[:,:,:],bt[:,q:q+1].broadcast_to([P,NB*K0,H0]),ALU.mult)
                step(i)
                for q in range(3):
                    for h in range(2):
                        r=slice(h*DH,(h+1)*DH)
                        i=nc.vector.tensor_reduce(out=bias[r,:,q,:],in_=term[r,q].rearrange("p (b n h) e -> p b n h e",n=NP0,h=2)[:,:,:,h],axis=mybir.AxisListType.X,op=ALU.add)
                step(i)
        w=sb("w",[P,2,2,2,3*K0*DH],F16); wst=sb("wst",[P,2,3*K0*DH])
        c=Core(); c.pairs=NP0; c.tiles=[(P,0,t*T) for t in range(4)]; c.pcols=4*T; c.rope=False; c.pm=0; c.w=w; c.wo=wo; c.mask=mask; c.ones=ones; c.identb=identb; c.name='picked'
        c.bo=bo_s
        c.batch_per_turn=2; c.h_buffers=2; c.v_buffers=2; c.w_of=lambda n: w[:,(n//NP0)%2]
        c.bias=lambda b,what,n: bias[:,bass.ds(b,1),what,n]
        c.gate=lambda b,n: gate[:,bass.ds(b,1),n]
        sel=ctx.enter_context(semaphores(nc,"sel_")); w_loaded=sel("w_loaded"); w_hi=sel("w_hi"); c.w_ready=sel("w_ready")
        def select(nc,block,ctx_,hi):
            @block.sync
            def _(sp):
                with sp.Fori(0,NB+2) as it:
                    sp.wait_ge(c.w_ready,it)
                    for kk in range(K0):
                        r=sp.value_load(idx[0:1,bass.ds((it%NB)*K0+kk,1)],min_val=0,max_val=H0-1)
                        for q,src in enumerate((Wq,Wk,Wv)):
                            at=q*K0*DH+kk*DH
                            sp.dma_start(wst[:,:,at:at+DH],src[:,bass.ds(r*DH,DH)].rearrange("(k p) n -> p k n",p=P)).then_inc(w_loaded,16)
        c.select=select
        def high_weights(act,b,n):
            act.wait_ge(w_loaded,(b+1)*16*3*K0)
            nc.scalar.activation(c.w_of(n)[:,0],wst[:,:,:],ACT.Copy).then_inc(w_hi,1)
        def low_weights(pool,b,n):
            pool.wait_ge(w_hi,b+1)
            nc.gpsimd.tensor_tensor(c.w_of(n)[:,1],wst[:,:,:],c.w_of(n)[:,0],ALU.subtract).then_inc(c.w_ready,1)
        c.high_weights=high_weights; c.low_weights=low_weights
        attention_core(nc,XT,HT,c)


def cond1_stage(nc, XT, HT, cond, base_up_T, base_down, ln_gamma, ln_beta, W1, bias1, w2, w2_in, W2, bias2, norm_weight, ident):
    BR=NB*RANK
    with ExitStack() as ctx:
        sb=lambda n,s,d=F32: ctx.enter_context(nc.sbuf_tensor("adapt_"+n,s,d))
        sem=ctx.enter_context(semaphores(nc,"adapt_"))
        up=sb("up",[P,2,D]); down=sb("down",[P,2,D]); mask=sb("mask",[BR,NB]); wT=sb("wT",[P,4,2,BR]); wR=sb("wR",[BR,2,D]); nw=sb("nw",[P,2]); eps=sb("eps",[P,1]); ones=sb("ones",[P,P])
        with ExitStack() as c1:
            sb1=lambda n,s,d=F32: c1.enter_context(nc.sbuf_tensor("gen_"+n,s,d))
            sem1=c1.enter_context(semaphores(nc,"gen_"))
            w2_last=sb1("w2_last",[P,2,D*RANK]); w1=sb1("w1",[P,2,D]); b1=sb1("b1",[P,2]); b2=sb1("b2",[P,4,2,RANK]); ga=sb1("gamma",[P,2]); be=sb1("beta",[P,2])
            c=sb1("c",[NB,D]); sq=sb1("sq",[NB,D]); st=sb1("stats",[NB,5]); cT=sb1("cT",[P,2,NB]); hT=sb1("hT",[P,2,NB])
            ps_c=c1.enter_context(nc.psum_tensor("gen_ps_c",[P,512],F32)); ps_h=c1.enter_context(nc.psum_tensor("gen_ps_h",[P,512],F32)); ps_w=c1.enter_context(nc.psum_tensor("gen_ps_w",[P,512],F32)); ps_r=c1.enter_context(nc.psum_tensor("gen_ps_r",[P,512],F32))
            cond_in=sem1("cond_in"); small_in=sem1("small_in"); last_in=sem1("last_in"); const=sem1("const"); dv=sem1("dv"); root=sem1("root"); turned=sem1("turned"); hid=sem1("hid"); gel=sem1("gel"); made=sem1("made"); rows=sem1("rows")
            block=c1.enter_context(nc.Block())
            @block.sync
            def _(sp):
                c1.enter_context(nc.allow_non_contiguous_dma(reason="a few small vectors"))
                sp.dma_start(c[:,:],cond).then_inc(cond_in,16)
                sp.dma_start(w1[:,:,:],W1.rearrange("(k p) n -> p k n",p=P)).then_inc(small_in,16)
                sp.dma_start(w2_last[:,:,:],W2[:,3*D*RANK:].rearrange("(k p) n -> p k n",p=P)).then_inc(last_in,16)
                for dst,src in ((b1,bias1),(ga,ln_gamma),(be,ln_beta),(nw,norm_weight)):
                    sp.dma_start(dst[:,:],src.rearrange("(k p) -> p k",p=P)).then_inc(small_in,16)
                for q in range(4): sp.dma_start(b2[:,q],bias2.rearrange("(q k p r) -> q p k r",q=4,k=2,r=RANK)[q]).then_inc(small_in,16)
                sp.dma_start(up[:,:,:],base_up_T.rearrange("(k p) n -> p k n",p=P)).then_inc(small_in,16)
                sp.dma_start(down[:,:,:],base_down.rearrange("(k p) n -> p k n",p=P)).then_inc(small_in,16)
            @block.gpsimd
            def _(pool):
                nc.gpsimd.memset(ones[:,:],1.0).then_inc(const,1)
                nc.gpsimd.memset(eps[:,:],float(np.finfo(np.float32).eps)).then_inc(const,1)
                nc.gpsimd.memset(st[:,4:5],1e-5).then_inc(const,1)
                nc.gpsimd.memset(mask[:,:],1.0).then_inc(const,1)
                pool.wait_ge(const,4)
                nc.gpsimd.affine_select(out=mask[:,:],in_=mask[:,:],compare_op=ALU.is_ge,fill=0.0,base=0,pattern=[[-RANK,NB]],channel_multiplier=1).then_inc(const,1)
                pool.wait_ge(const,5)
                nc.gpsimd.affine_select(out=mask[:,:],in_=mask[:,:],compare_op=ALU.is_ge,fill=0.0,base=RANK-1,pattern=[[RANK,NB]],channel_multiplier=-1).then_inc(const,1)
            @block.vector
            def _(dve):
                n=[0]
                def step(i):
                    n[0]+=1; i.then_inc(dv,1); dve.wait_ge(dv,n[0])
                dve.wait_ge(cond_in,16)
                X_=mybir.AxisListType.X
                step(nc.vector.tensor_reduce(out=st[:,0:1],in_=c[:,:],axis=X_,op=ALU.add))
                step(nc.vector.tensor_scalar(st[:,0:1],st[:,0:1],1.0/D,None,ALU.mult))
                step(nc.vector.tensor_scalar(c[:,:],c[:,:],st[:,0:1],None,ALU.subtract))
                step(nc.vector.tensor_tensor(sq[:,:],c[:,:],c[:,:],ALU.mult))
                step(nc.vector.tensor_reduce(out=st[:,1:2],in_=sq[:,:],axis=X_,op=ALU.add))
                dve.wait_ge(root,1)
                step(nc.vector.reciprocal(st[:,3:4],st[:,2:3]))
                step(nc.vector.tensor_scalar(c[:,:],c[:,:],st[:,3:4],None,ALU.mult))
                dve.wait_ge(turned,1); dve.wait_ge(small_in,16*11)
                for k in range(2): step(nc.vector.tensor_scalar(cT[:,k],ps_c[:,k*NB:(k+1)*NB],ga[:,k:k+1],be[:,k:k+1],ALU.mult,ALU.add))
                dve.wait_ge(made,1)
                for q in range(4):
                    for k in range(2):
                        at=(q*2+k)*BR
                        i=nc.vector.tensor_tensor(wT[:,q,k,:].rearrange("p (b r) -> p b r",r=RANK),ps_w[:,at:at+BR].rearrange("p (r b) -> p b r",b=NB),b2[:,q,k:k+1,:].broadcast_to([P,NB,RANK]),ALU.add)
                step(i)
                dve.wait_ge(rows,1)
                step(nc.vector.tensor_copy(wR[:,:,:],ps_r[0:BR,:].rearrange("p (q d) -> p q d",q=2)))
            @block.scalar
            def _(act):
                act.wait_ge(dv,5); act.wait_ge(const,3)
                nc.scalar.activation(st[:,2:3],st[:,1:2],ACT.Sqrt,scale=1.0/D,bias=st[:,4:5]).then_inc(root,1)
                act.wait_ge(hid,1)
                for k in range(2): i=nc.scalar.activation(hT[:,k],ps_h[:,k*NB:(k+1)*NB],ACT.Gelu,bias=b1[:,k:k+1])
                i.then_inc(gel,1)
            @block.tensor
            def _(pe):
                pe.wait_ge(dv,7)
                for k in range(2): i=nc.tensor.transpose(ps_c[:,k*NB:(k+1)*NB],c[:,k*P:(k+1)*P],ident[0:NB,0:NB])
                i.then_inc(turned,1)
                pe.wait_ge(dv,9)
                for o in range(2):
                    for k in range(2): i=nc.tensor.matmul(ps_h[:,o*NB:(o+1)*NB],w1[:,k,o*P:(o+1)*P],cT[:,k],start=(k==0),stop=(k==1))
                i.then_inc(hid,1)
                pe.wait_ge(gel,1)
                pe.wait_ge(w2_in,32); pe.wait_ge(last_in,16)
                for q in range(4):
                    for o in range(2):
                        for r in range(RANK):
                            for k in range(2):
                                at=((q*2+o)*RANK+r)*NB
                                i=nc.tensor.matmul(ps_w[:,at:at+NB],(w2[:,k,q*D*RANK:(q+1)*D*RANK] if q<3 else w2_last[:,k]).rearrange("p (d r) -> p d r",r=RANK)[:,o*P:(o+1)*P,r],hT[:,k],start=(k==0),stop=(k==1))
                i.then_inc(made,1)
                pe.wait_ge(dv,10)
                for j,q in enumerate((0,3)):
                    for o in range(2): i=nc.tensor.transpose(ps_r[0:BR,j*D+o*P:j*D+(o+1)*P],wT[:,q,o,:],ident[:,:])
                i.then_inc(rows,1)
        u=sb("u",[BR,T]); v=sb("v",[BR,T]); mid=sb("mid",[P,2,T]); sq=sb("sq",[P,2,2,T]); rs=sb("rs",[P,2,T]); rr=sb("rr",[P,2,T])
        ps_u=ctx.enter_context(nc.psum_tensor("adapt_ps_u",[P,512],F32)); ps_v=ctx.enter_context(nc.psum_tensor("adapt_ps_v",[P,512],F32)); ps_m=ctx.enter_context(nc.psum_tensor("adapt_ps_m",[P,2,512],F32)); ps_o=ctx.enter_context(nc.psum_tensor("adapt_ps_o",[P,2,512],F32)); ps_n=ctx.enter_context(nc.psum_tensor("adapt_ps_n",[P,2,512],F32))
        u_done,u_kept,mid_done,gelled,v_done,v_kept,o_done,added,squared,summed,rooted,inverted,scaled=[sem(n) for n in "u_done,u_kept,mid_done,gelled,v_done,v_kept,o_done,added,squared,summed,rooted,inverted,scaled".split(",")]
        block=ctx.enter_context(nc.Block())
        def at_b(X,k,it): return X[:,k,bass.ds(it,1),:].rearrange("p a t -> p (a t)")
        @block.tensor
        def _(pe):
            with pe.Fori(0,NB) as it:
                pe.wait_ge(u_kept,it)
                for k in range(2): i=nc.tensor.matmul(ps_u[0:BR,:],wT[:,2,k,:],at_b(XT,k,it),start=(k==0),stop=(k==1))
                i.then_inc(u_done,1)
                pe.wait_ge(gelled,it)
                for o in range(2):
                    for k in range(2): nc.tensor.matmul(ps_m[:,o,:],down[:,k,o*P:(o+1)*P],at_b(XT,k,it),start=(k==0),stop=False)
                pe.wait_ge(u_kept,it+1)
                for o in range(2): i=nc.tensor.matmul(ps_m[:,o,:],wR[:,1,o*P:(o+1)*P],u[:,:],start=False,stop=True)
                i.then_inc(mid_done,1)
                pe.wait_ge(gelled,it+1)
                for k in range(2): i=nc.tensor.matmul(ps_v[0:BR,:],wT[:,1,k,:],mid[:,k],start=(k==0),stop=(k==1))
                i.then_inc(v_done,1)
                pe.wait_ge(added,it)
                for o in range(2):
                    for k in range(2): nc.tensor.matmul(ps_o[:,o,:],up[:,k,o*P:(o+1)*P],mid[:,k],start=(k==0),stop=False)
                pe.wait_ge(v_kept,it+1)
                for o in range(2): i=nc.tensor.matmul(ps_o[:,o,:],wR[:,0,o*P:(o+1)*P],v[:,:],start=False,stop=True)
                i.then_inc(o_done,1)
            with pe.Fori(0,NB//2) as it:
                for j in range(2):
                    pe.wait_ge(squared,it*2+j+1)
                    pe.wait_ge(rooted,it*2+j)
                    for k in range(2): i=nc.tensor.matmul(ps_n[:,j,:],ones[:,:],sq[:,j,k],start=(k==0),stop=(k==1))
                    i.then_inc(summed,1)
        @block.vector
        def _(dve):
            with dve.Fori(0,NB) as it:
                dve.wait_ge(u_done,it+1)
                nc.vector.tensor_scalar(u[:,:],ps_u[0:BR,:],mask[:,bass.ds(it,1)],None,ALU.mult).then_inc(u_kept,1)
                dve.wait_ge(v_done,it+1)
                nc.vector.tensor_scalar(v[:,:],ps_v[0:BR,:],mask[:,bass.ds(it,1)],None,ALU.mult).then_inc(v_kept,1)
                dve.wait_ge(o_done,it+1)
                for k in range(2): i=nc.vector.tensor_tensor(at_b(HT,k,it),ps_o[:,k,:],at_b(XT,k,it),ALU.add)
                i.then_inc(added,1)
            with dve.Fori(0,NB//2) as it:
                for j in range(2):
                    dve.wait_ge(rooted,it*2+j+1)
                    nc.vector.reciprocal(rr[:,j],rs[:,j]).then_inc(inverted,1)
                    dve.wait_ge(inverted,it*2+j+1)
                    for k in range(2):
                        y=at_b(HT,k,it*2+j)
                        nc.vector.scalar_tensor_tensor(out=y,in0=y,scalar=nw[:,k:k+1],in1=rr[:,j],op0=ALU.mult,op1=ALU.mult).then_inc(scaled,1)
        @block.scalar
        def _(act):
            with act.Fori(0,NB) as it:
                act.wait_ge(mid_done,it+1)
                act.wait_ge(o_done,it)
                for k in range(2): i=nc.scalar.activation(mid[:,k],ps_m[:,k,:],ACT.Gelu)
                i.then_inc(gelled,1)
            act.wait_ge(added,NB)
            with act.Fori(0,NB//2) as it:
                for j in range(2):
                    act.wait_ge(summed,it*2+j) if j==0 else act.wait_ge(summed,it*2+j-1)
                    for k in range(2): i=nc.scalar.activation(sq[:,j,k],at_b(HT,k,it*2+j),ACT.Square)
                    i.then_inc(squared,1)
                for j in range(2):
                    act.wait_ge(summed,it*2+j+1)
                    act.wait_ge(inverted,it*2+j)
                    nc.scalar.activation(rs[:,j],ps_n[:,j,:],ACT.Sqrt,scale=1.0/D,bias=eps[:,0:1]).then_inc(rooted,1)


def rnn_stage(nc, XT, HT, Wx, Wh, bias, h0T, T=T):
    with ExitStack() as ctx:
        sb=lambda n,s,d=F32: ctx.enter_context(nc.sbuf_tensor("rnn_"+n,s,d))
        sem=ctx.enter_context(semaphores(nc,"rnn_"))
        NIT=T//(2*C); W=C//2*NB
        banks=ctx.enter_context(nc.psum_tensor("rnn_banks",[P,2,2,512],F32))
        wx=sb("wx",[P,2,D]); wh=sb("wh",[P,2,D]); b=sb("b",[1,D])
        xs=sb("xs",[P,2,2,2,2,C//2,NB],F16)
        xf=sb("xf",[P,2,2,C//2,NB]); zeros=sb("zeros",[P,C//2,NB])
        wxp=sb("wxp",[P,2,2,D],F16); whp=sb("whp",[P,2,2,D],F16); bp=sb("bp",[1,2,D],F16)
        hp=sb("hp",[P,2,2,NB],F16); hist=sb("hist",[P,2,2*C,NB]); ones=sb("ones",[1,W],F16)
        loaded=sem("loaded"); init=sem("init"); zeroed=sem("zeroed"); wsplit=sem("wsplit"); h0split=sem("h0split")
        x_fp32=sem("x_fp32"); x_hi=sem("x_hi"); x_staged=sem("x_staged"); x_projected=sem("x_projected")
        pre_ready=sem("pre_ready"); hi_ready=sem("hi_ready"); h_fp32=sem("h_fp32"); h_ready=sem("h_ready"); hist_saved=sem("hist_saved")
        def pre(st,par): return banks[:,st,par,0:2*W].rearrange("p (u s b) -> p u s b",u=2,b=NB)
        block=ctx.enter_context(nc.Block())
        @block.sync
        def _(sp):
            sp.dma_start(wx[:,:,:],Wx.rearrange("(k p) n -> p k n",p=P)).then_inc(loaded,16)
            sp.dma_start(wh[:,:,:],Wh.rearrange("(k p) n -> p k n",p=P)).then_inc(loaded,16)
            sp.dma_start(b[0:1,:],bias.rearrange("(a n) -> a n",a=1)).then_inc(loaded,16)
        @block.gpsimd
        def _(pool):
            nc.gpsimd.memset(ones[:,:],1.0).then_inc(init,1)
            nc.gpsimd.memset(zeros[:,:,:],0.0).then_inc(zeroed,1)
            pool.wait_ge(zeroed,1)
            pool.sem_inc(hist_saved,4)
            def stage(st,half,before=0):
                n=0
                for par in range(2):
                    for k in range(2):
                        src=XT[:,k,:,:].rearrange("p b (s q) -> p q s b",q=2)[:,par]
                        n+=1
                        nc.gpsimd.tensor_copy(xf[:,k,par], src[:,bass.ds(half,C//2),:]).then_inc(x_fp32,1)
                        pool.wait_ge(x_fp32, before+n)
                        nc.gpsimd.tensor_tensor(xs[:,st,0,k,par], xf[:,k,par], zeros[:,:,:], ALU.add).then_inc(x_hi,1)
                        pool.wait_ge(x_hi, before+n)
                        nc.gpsimd.tensor_tensor(xs[:,st,1,k,par], xf[:,k,par], xs[:,st,0,k,par], ALU.subtract).then_inc(x_staged,1)
            stage(0,0)
            with pool.Fori(0,NIT) as it:
                for st in range(2):
                    pool.wait_ge(x_projected, it*2+st+1)
                    stage(1-st, it*C+C//2 if st==0 else (it*C+C)%(T//2), it*8+4*(st+1))
                    pool.wait_ge(h_ready, it*2*C+C*(st+1))
                    for u in range(2):
                        nc.gpsimd.tensor_copy(HT[:,u,:,bass.ds(it*2*C+st*C,C)].rearrange("p b t -> p t b"), hist[:,u,st*C:(st+1)*C,:]).then_inc(hist_saved,1)
        @block.tensor
        def _(pe):
            def project(st,par,tiles=(0,1)):
                for u in tiles:
                    for part in range(2):
                        nc.tensor.matmul(pre(st,par)[:,u], bp[0:1,part,u*P:u*P+P], ones[0:1,:], start=(u==0 and part==0),stop=False,skip_group_check=True)
                    for k in range(2):
                        for wpart,xpart in ((0,0),(1,0),(0,1)):
                            last=nc.tensor.matmul(pre(st,par)[:,u], wxp[:,wpart,k,u*P:u*P+P], xs[:,st,xpart,k,par], start=False,stop=False,skip_group_check=True)
                return last
            pe.wait_ge(init,1); pe.wait_ge(wsplit,6); pe.wait_ge(h0split,4); pe.wait_ge(x_staged,4)
            project(0,0)
            project(0,1).then_inc(x_projected,1)
            with pe.Fori(0,NIT) as it:
                for s in range(2*C):
                    st,cs=divmod(s,C); par=cs%2; j=cs//2
                    for hpart,ready,wparts in ((0,hi_ready,(0,1)),(1,h_ready,(0,))):
                        pe.wait_ge(ready, it*2*C+s)
                        for k in range(2):
                            for u in range(2):
                                for wpart in wparts:
                                    last=nc.tensor.matmul(pre(st,par)[:,u,j], whp[:,wpart,k,u*P:u*P+P], hp[:,k,hpart], start=False,stop=True,skip_group_check=True)
                    last.then_inc(pre_ready,1)
                    if cs>=8 and cs%2==0:
                        if cs==8: pe.wait_ge(x_staged, it*8+4*(st+2))
                        last=project(1-st,(cs-8)//4,((cs//2)%2,))
                        if cs==14: last.then_inc(x_projected,1)
        @block.scalar
        def _(act):
            with act.Fori(0,NIT) as it:
                for s in range(2*C):
                    st,cs=divmod(s,C); par=cs%2; j=cs//2
                    act.wait_ge(pre_ready, it*2*C+s+1)
                    nc.scalar.activation(hp[:,:,0], pre(st,par)[:,:,j], ACT.Tanh).then_inc(hi_ready,1)
                    if cs==0: act.wait_ge(hist_saved, it*4+2*st+2)
                    nc.scalar.activation(hist[:,:,s], pre(st,par)[:,:,j], ACT.Tanh).then_inc(h_fp32,1)
        @block.vector
        def _(dve):
            dve.wait_ge(loaded,48)
            for n,(src,dst) in enumerate(((wx[:,:,:],wxp),(wh[:,:,:],whp),(b[0:1,:],bp))):
                hi,lo=dst[:,0],dst[:,1]
                nc.vector.tensor_copy(hi,src).then_inc(wsplit,1)
                dve.wait_ge(wsplit,2*n+1)
                nc.vector.tensor_tensor(lo,src,hi,ALU.subtract).then_inc(wsplit,1)
            for k in range(2):
                nc.vector.tensor_copy(hp[:,k,0],h0T[:,k]).then_inc(h0split,1)
                dve.wait_ge(h0split,2*k+1)
                nc.vector.tensor_tensor(hp[:,k,1],h0T[:,k],hp[:,k,0],ALU.subtract).then_inc(h0split,1)
            with dve.Fori(0,NIT) as it:
                for s in range(2*C):
                    dve.wait_ge(h_fp32, it*2*C+s+1)
                    nc.vector.tensor_tensor(hp[:,:,1], hist[:,:,s], hp[:,:,0], ALU.subtract).then_inc(h_ready,1)


def moe_stage(nc, XT, HT, gate_w, gate_b, swg, swu, swd, ewg, ewu, ewd, ident, out):
    TT=T//P
    with ExitStack() as ctx:
        sb=lambda n,s,d=F32: ctx.enter_context(nc.sbuf_tensor("moe_"+n,s,d))
        sem=ctx.enter_context(semaphores(nc,"moe_"))
        wgp=sb("wgp",[P,2,2,NX,I],F16); wup=sb("wup",[P,2,2,NX,I],F16); wdp=sb("wdp",[P,2,NX,D],F16)
        gT=sb("gT",[48,NB,T],BF16)
        sel=sb("sel",[48,NE,P],BF16)
        with ExitStack() as c1:
            sb1=lambda n,s,d=F32: c1.enter_context(nc.sbuf_tensor("route_"+n,s,d))
            sem1=c1.enter_context(semaphores(nc,"route_"))
            wst=sb1("wst",[P,2,3,4*2*I])
            gw=sb1("gw",[P,2,NE]); gb=sb1("gb",[NE,1]); iota=sb1("iota",[P,TT,NE]); iota_i=sb1("iota_i",[P,TT,NE],mybir.dt.int32)
            identb=sb1("identb",[P,P],BF16)
            sg=sb1("sg",[NE,T]); sv=sb1("sv",[P,TT,NE]); top=sb1("top",[P,TT,8]); topi=sb1("topi",[P,TT,8],U32); topf=sb1("topf",[P,TT,8])
            tot=sb1("tot",[P,TT]); oh=sb1("oh",[P,2,TT,NE]); g32=sb1("g32",[P,TT,NE]); rest=sb1("rest",[P,TT,NE]); gp=sb1("gp",[P,TT,3,NE],BF16)
            pl=c1.enter_context(nc.psum_tensor("route_logits",[P,512],F32)); pt=c1.enter_context(nc.psum_tensor("route_tok",[P,512],F32)); pb=c1.enter_context(nc.psum_tensor("route_back",[P,1024],BF16))
            loaded=[sem1(f"loaded{i}") for i in range(2)]; gl=sem1("gate_loaded"); hi_done=sem1("hi_done"); lo_done=sem1("lo_done")
            const=sem1("const"); zeroed=sem1("zeroed"); logits=sem1("logits"); sig=sem1("sig"); tok=sem1("tok"); dv=sem1("dv"); parts=sem1("parts"); back=sem1("back"); kept=sem1("kept"); idb=sem1("idb"); pe_passed=sem1("pe_passed"); dve_passed=sem1("dve_passed")
            block=c1.enter_context(nc.Block())
            groups=[[4*i+j for j in range(4)] for i in range(NE//4)]+[[NE]]
            def pieces(gi):
                grp=groups[gi]; n=len(grp); s=gi%2
                for q,(dst,K) in enumerate(((wgp,2),(wup,2),(wdp,0))):
                    if K: yield q, wst[:,s,q,0:2*n*I].rearrange("p (k e i) -> p k e i",k=2,i=I), (dst[:,0,:,grp[0]:grp[0]+n],dst[:,1,:,grp[0]:grp[0]+n])
                    else: yield q, wst[:,s,q,0:n*D].rearrange("p (e i) -> p e i",i=D), (dst[:,0,grp[0]:grp[0]+n],dst[:,1,grp[0]:grp[0]+n])
            @block.sync
            def _(sp):
                sp.dma_start(gw[:,:,:],gate_w.rearrange("(k p) n -> p k n",p=P)).then_inc(gl,16)
                sp.dma_start(gb[:,:],gate_b.rearrange("(n a) -> n a",a=1)).then_inc(gl,16)
                for gi,grp in enumerate(groups):
                    if gi>=2: sp.wait_ge(lo_done,3*(gi-1))
                    for q,st,_ in pieces(gi):
                        if grp[0]==NE:
                            src=(swg,swu,swd)[q]
                            if q<2:
                                sp.dma_start(st[:,:,0,:],src.rearrange("(k p) i -> p k i",p=P)).then_inc(loaded[gi%2],16)
                            else: sp.dma_start(st[:,0,:],src).then_inc(loaded[gi%2],16)
                        else:
                            src=(ewg,ewu,ewd)[q][grp[0]:grp[0]+len(grp)]
                            if q<2:
                                for k in range(2):
                                    sp.dma_start(st[:,k],src[:,k*P:(k+1)*P,:].rearrange("e p i -> p e i")).then_inc(loaded[gi%2],16)
                            else: sp.dma_start(st,src.rearrange("e i d -> i e d")).then_inc(loaded[gi%2],16)
            @block.gpsimd
            def _(pool):
                nc.gpsimd.iota(iota_i[:,:,:],pattern=[[0,TT],[1,NE]],base=0,channel_multiplier=0).then_inc(const,1)
                nc.gpsimd.memset(sel[:,:,:],0.0).then_inc(zeroed,1)
                pool.wait_ge(zeroed,1)
                for part in range(3):
                    nc.gpsimd.affine_select(out=sel[:,:,:],in_=sel[:,:,:],compare_op=ALU.not_equal,fill=1.0,base=-NE*part,pattern=[[-1,NE],[0,P]],channel_multiplier=1).then_inc(zeroed,1)
                    pool.wait_ge(zeroed,2+part)
                n=0
                for gi in range(len(groups)):
                    for q,st,(hi,lo) in pieces(gi):
                        n+=1
                        pool.wait_ge(hi_done,n)
                        if q<2:
                            for k in range(2):
                                i=nc.gpsimd.tensor_tensor(lo[:,k],st[:,k],hi[:,k],ALU.subtract)
                            i.then_inc(lo_done,1)
                        else: nc.gpsimd.tensor_tensor(lo,st,hi,ALU.subtract).then_inc(lo_done,1)
            @block.tensor
            def _(pe):
                pe.wait_ge(gl,32)
                pe.wait_ge(idb,1)
                with pe.Fori(0,NB) as it:
                    pe.wait_ge(sig,it)
                    for k in range(2):
                        last=nc.tensor.matmul(pl[0:NE,:],gw[:,k,:],HT[:,k,bass.ds(it,1),:].rearrange("p a t -> p (a t)"),start=(k==0),stop=(k==1))
                    last.then_inc(logits,1)
                    pe.wait_ge(sig,it+1)
                    pe.sem_inc(pe_passed,1)
                    for j in range(TT):
                        last=nc.tensor.transpose(pt[:,j*NE:(j+1)*NE],sg[:,j*P:(j+1)*P],ident[0:NE,0:NE])
                    last.then_inc(tok,1)
                    pe.wait_ge(parts,it+1)
                    pe.sem_inc(pe_passed,1)
                    for j in range(TT):
                        last=nc.tensor.transpose(pb[0:48,j*P:(j+1)*P],gp[:,j].rearrange("p a e -> p (a e)"),identb[:,:])
                    last.then_inc(back,1)
            @block.scalar
            def _(act):
                for gi in range(len(groups)):
                    act.wait_ge(loaded[gi%2],16*5*(gi//2)+16*(3 if gi==len(groups)-1 else 5))
                    for q,st,(hi,lo) in pieces(gi):
                        nc.scalar.activation(hi,st,ACT.Copy).then_inc(hi_done,1)
                act.wait_ge(gl,32)
                with act.Fori(0,NB) as it:
                    act.wait_ge(tok,it)
                    act.wait_ge(logits,it+1)
                    nc.scalar.activation(sg[:,:],pl[0:NE,:],ACT.Sigmoid,bias=gb[:,0:1]).then_inc(sig,1)
                    act.wait_ge(back,it+1)
                    nc.scalar.activation(gT[:,bass.ds(it,1),:].rearrange("p a t -> p (a t)"),pb[0:48,0:T],ACT.Copy).then_inc(kept,1)
            @block.vector
            def _(dve):
                dve.wait_ge(const,1)
                nc.vector.tensor_copy(identb[:,:],ident[:,:]).then_inc(idb,1)
                nc.vector.tensor_copy(iota[:,:,:],iota_i[:,:,:]).then_inc(dv,1)
                dve.wait_ge(dv,1)
                steps=TT+TT+8
                with dve.Fori(0,NB) as it:
                    n=[0]
                    def done(i): n[0]+=1; i.then_inc(dv,1)
                    def after(): dve.wait_ge(dv,it*(2*TT+12)+n[0]+1)
                    dve.wait_ge(tok,it+1)
                    dve.wait_ge(back,it)
                    done(nc.vector.tensor_copy(sv[:,:,:],pt[:,0:TT*NE].rearrange("p (a e) -> p a e",e=NE))); after()
                    dve.sem_inc(dve_passed,1)
                    for j in range(TT): done(nc.vector.max(top[:,j],sv[:,j]))
                    after()
                    dve.sem_inc(dve_passed,1)
                    for j in range(TT): done(nc.vector.max_index(topi[:,j],top[:,j],sv[:,j]))
                    done(nc.vector.tensor_tensor(tot[:,:],top[:,:,0],top[:,:,1],ALU.add)); after()
                    done(nc.vector.tensor_copy(topf[:,:,:],topi[:,:,:])); 
                    done(nc.vector.reciprocal(tot[:,:],tot[:,:])); after()
                    for c in range(2):
                        done(nc.vector.tensor_tensor(oh[:,c],iota[:,:,:],topf[:,:,c:c+1].broadcast_to([P,TT,NE]),ALU.is_equal))
                    after()
                    done(nc.vector.tensor_tensor(oh[:,0],oh[:,0],oh[:,1],ALU.add)); after()
                    done(nc.vector.tensor_tensor(oh[:,0],oh[:,0],sv[:,:,:],ALU.mult)); after()
                    done(nc.vector.tensor_tensor(g32[:,:,:],oh[:,0],tot[:,:].rearrange("p (a o) -> p a o",o=1).broadcast_to([P,TT,NE]),ALU.mult)); after()
                    done(nc.vector.tensor_copy(gp[:,:,0],g32[:,:,:])); after()
                    done(nc.vector.tensor_tensor(rest[:,:,:],g32[:,:,:],gp[:,:,0],ALU.subtract)); after()
                    nc.vector.tensor_copy(gp[:,:,1],rest[:,:,:]).then_inc(dv,1); n[0]+=1; after()
                    nc.vector.tensor_tensor(gp[:,:,2],rest[:,:,:],gp[:,:,1],ALU.subtract).then_inc(parts,1)
                    assert n[0]==2*TT+12,n[0]
        with ExitStack() as c2:
            sb2=lambda n,s,d=F32: c2.enter_context(nc.sbuf_tensor("exp_"+n,s,d))
            sem2=c2.enter_context(semaphores(nc,"exp_"))
            ph=[c2.enter_context(nc.psum_tensor(f"exp_hg{i}",[P,512],F32)) for i in range(2)]
            pu=[c2.enter_context(nc.psum_tensor(f"exp_hu{i}",[P,512],F32)) for i in range(2)]
            pg=[c2.enter_context(nc.psum_tensor(f"exp_gate{i}",[P,512],F32)) for i in range(2)]
            pa=c2.enter_context(nc.psum_tensor("exp_acc",[P,2,512],F32))
            hs=sb2("hs",[P,2,2,T],F16)
            res=sb2("res",[P,2,T])
            si=sb2("silu",[P,2,T]); tu=sb2("tu",[P,2,T]); tg=sb2("tg",[P,2,T]); hid=sb2("hid",[P,2,2,T],F16)
            ob=sb2("ob",[P,2,512])
            hs_hi,hs_ready,res_ready,hg,hu,gt,silu,up,gated,hi,lo,down,summed,stored,ob_ready,resid=[sem2(n) for n in "hs_hi,hs_ready,res_ready,hg,hu,gt,silu,up,gated,hi,lo,down,summed,stored,ob_ready,resid".split(",")]
            pe_passed2=sem2("pe_passed")
            block=c2.enter_context(nc.Block())
            def slot_free(eng,s,it,e):
                eng.wait_ge(s, it*NX+(e-1 if e>=2 else 0))
            @block.gpsimd
            def _(pool):
                with pool.Fori(0,NB) as it:
                    pool.wait_ge(summed,it)
                    for k in range(2):
                        nc.gpsimd.tensor_tensor(res[:,k],XT[:,k,bass.ds(it,1),:].rearrange("p a t -> p (a t)"),HT[:,k,bass.ds(it,1),:].rearrange("p a t -> p (a t)"),ALU.add).then_inc(res_ready,1)
                    for e in range(NX):
                        pool.wait_ge(hi,it*NX+e+1)
                        nc.gpsimd.tensor_tensor(hid[:,e%2,1],tg[:,e%2],hid[:,e%2,0],ALU.subtract).then_inc(lo,1)
            @block.tensor
            def _(pe):
                with pe.Fori(0,NB) as it:
                    def mm3(out,w,x,**kw):
                        pass
                    def upward(e):
                        s=e%2
                        slot_free(pe,silu,it,e)
                        for pp,w,q in ((ph,wgp,hg),(pu,wup,hu)):
                            if q is hu: slot_free(pe,up,it,e)
                            n=0
                            for k in range(2):
                                for wpart,xpart in ((0,0),(1,0),(0,1)):
                                    last=nc.tensor.matmul(pp[s][:,:],w[:,wpart,k,e],hs[:,xpart,k],start=(n==0),stop=(n==5)); n+=1
                            last.then_inc(q,1)
                        if e<NE:
                            pe.wait_ge(gated, it*NX+(e-1 if e>=2 else 0))
                            pe.sem_inc(pe_passed2,1)
                            nc.tensor.matmul(pg[s][:,:],sel[:,e],gT[:,bass.ds(it,1),:].rearrange("p a t -> p (a t)"),start=True,stop=True).then_inc(gt,1)
                    def downward(e):
                        pe.wait_ge(hi,it*NX+e+1)
                        pe.wait_ge(lo,it*NX+e+1)
                        for tt in range(TT):
                            for wpart,xpart in ((0,0),(1,0),(0,1)):
                                last=nc.tensor.matmul(pa[:,tt//2,(tt%2)*D:(tt%2+1)*D],hid[:,e%2,xpart,tt*P:(tt+1)*P],wdp[:,wpart,e],start=False,stop=(e==NE),skip_group_check=True)
                        last.then_inc(down,1)
                    pe.wait_ge(hs_ready,it*2+2)
                    upward(0)
                    pe.wait_ge(summed,it)
                    pe.wait_ge(res_ready,it*2+2)
                    for tt in range(TT):
                        for k in range(2):
                            last=nc.tensor.matmul(pa[:,tt//2,(tt%2)*D+k*P:(tt%2)*D+(k+1)*P],res[:,k,tt*P:(tt+1)*P],ident[:,:],start=(tt%2==0 and k==0),stop=False,skip_group_check=True)
                    last.then_inc(resid,1)
                    for e in range(NE):
                        upward(e+1)
                        downward(e)
                    downward(NE)
            @block.scalar
            def _(act):
                with act.Fori(0,NB) as it:
                    for e in range(NX):
                        s=e%2
                        act.wait_ge(hg,it*NX+e+1)
                        slot_free(act,up,it,e)
                        nc.scalar.activation(si[:,s],ph[s][:,:],ACT.Silu).then_inc(silu,1)
                        act.wait_ge(gated,it*NX+e+1)
                        slot_free(act,down,it,e)
                        nc.scalar.activation(hid[:,s,0],tg[:,s],ACT.Copy).then_inc(hi,1)
            @block.vector
            def _(dve):
                with dve.Fori(0,NB) as it:
                    dve.wait_ge(down,it*NX)
                    for k in range(2):
                        src=HT[:,k,bass.ds(it,1),:].rearrange("p a t -> p (a t)")
                        nc.vector.tensor_copy(hs[:,0,k],src).then_inc(hs_hi,1)
                        dve.wait_ge(hs_hi,it*2+k+1)
                        nc.vector.tensor_tensor(hs[:,1,k],src,hs[:,0,k],ALU.subtract).then_inc(hs_ready,1)
                    for e in range(NX):
                        s=e%2
                        dve.wait_ge(silu,it*NX+e+1)
                        dve.wait_ge(hu,it*NX+e+1)
                        slot_free(dve,gated,it,e)
                        if e<NE:
                            nc.vector.tensor_tensor(tu[:,s],si[:,s],pu[s][:,:],ALU.mult).then_inc(up,1)
                            dve.wait_ge(up,it*NX+e+1)
                            dve.wait_ge(gt,it*NE+e+1)
                            slot_free(dve,lo,it,e)
                            slot_free(dve,hi,it,e)
                            nc.vector.tensor_tensor(tg[:,s],tu[:,s],pg[s][:,:],ALU.mult).then_inc(gated,1)
                        else:
                            slot_free(dve,lo,it,e)
                            slot_free(dve,hi,it,e)
                            nc.vector.tensor_tensor(tg[:,s],si[:,s],pu[s][:,:],ALU.mult).then_inc(gated,1)
                            dve.wait_ge(gated,it*NX+e+1)
                            nc.vector.memset(tu[:,0,0:1],0.0).then_inc(up,1)
                    dve.wait_ge(down,it*NX+NX)
                    dve.wait_ge(stored,it*16)
                    nc.vector.tensor_copy(ob[:,:,:],pa[:,:,:]).then_inc(summed,1)
            @block.sync
            def _(sp):
                with sp.Fori(0,NB) as it:
                    sp.wait_ge(summed,it+1)
                    sp.dma_start(out[bass.ds(it,1)].rearrange("a (j q) d -> q (a j) d",q=P),ob[:,:,:].rearrange("p a (c d) -> p (a c) d",d=D)).then_inc(stored,16)
                sp.wait_ge(stored,16*NB)


def load_lstm_weights(nc, wx, wh, bias, Wx, Wh, b):
    with ExitStack() as ctx:
        sem=ctx.enter_context(semaphores(nc,"lstm_")); loaded=sem("loaded"); doubled=sem("doubled")
        block=ctx.enter_context(nc.Block())
        @block.sync
        def _(sp):
            sp.dma_start(wx[:,:,:],Wx.rearrange("(k p) n -> p k n",p=P)).then_inc(loaded,16)
            sp.dma_start(wh[:,:,:],Wh.rearrange("(k p) n -> p k n",p=P)).then_inc(loaded,16)
            sp.dma_start(bias[:,:],b.rearrange("(a n) -> a n",a=1)).then_inc(loaded,16)
        @block.vector
        def _(dve):
            dve.wait_ge(loaded,48)
            for w in (wx[:,:,3*NH:4*NH],wh[:,:,3*NH:4*NH],bias[:,3*NH:4*NH]): nc.vector.tensor_scalar(w,w,2.0,None,ALU.mult).then_inc(doubled,1)
            dve.wait_ge(doubled,3)
def build(nc, a, out):
    with ExitStack() as ctx:
        sb=lambda n,s,d=F32: ctx.enter_context(nc.sbuf_tensor(n,s,d))
        XT=sb("XT",[P,2,NB,T]); HT=sb("HT",[P,2,NB,T]); ident=sb("ident",[P,P]); h0T=sb("h0T",[P,2,NB])
        taps_dram=nc.dram_tensor("taps_scratch",[LH,P,P-1+WIN],F32).ap(); cols_dram=nc.dram_tensor("cols_scratch",[EDGES],F16).ap()
        g_dram=nc.dram_tensor("gates_scratch",[NB,K0],F32).ap(); i_dram=nc.dram_tensor("picked_scratch",[NB,K0],mybir.dt.int32).ap()
        make_ident(nc,ident)
        with ExitStack() as c:
            sb0=lambda n,s: c.enter_context(nc.sbuf_tensor(n,s,F32))
            wqkv=sb0("lm_wqkv",[P,2,3*LI]); out_w=sb0("lm_out_w",[P,LP,D]); out_b=sb0("lm_out_b",[P,2]); xg=sb0("xg",[P,2,T])
            dense_stage(nc,XT,HT,a["x"],a["xT"],a["condT"],a["L0_cond_weightT"],h0T,[
                (wqkv[:,:,:],a["L0_attn_qkv_w"].rearrange("(k p) n -> p k n",p=P)),
                (out_w[:,:,:],a["L0_attn_out_w"].rearrange("(k p) n -> p k n",p=P)),
                (out_b[:,:],a["L0_attn_out_b"].rearrange("(k p) -> p k",p=P))])
            nystrom_stage(nc,HT,wqkv,out_w,out_b,a["L0_attn_taps"],xg,ident,taps_dram)
            adjacency_stage(nc,XT,HT,xg,a["adj_rowsT"],a["L0_attn_adj_cols"],a["adj_valsT"],a["L0_attn_wq"],a["L0_attn_wk"],a["L0_attn_wv_w"],a["L0_attn_wv_b"],cols_dram)
        with ExitStack() as c:
            sb0=lambda n,s: c.enter_context(nc.sbuf_tensor(n,s,F32))
            wx=sb0("lstm_wx",[P,2,4*NH]); wh=sb0("lstm_wh",[P,2,4*NH]); bias=sb0("lstm_bias",[1,4*NH])
            load_lstm_weights(nc,wx,wh,bias,a["L0_cond2_Wx"],a["L0_cond2_Wh"],a["L0_cond2_b"])
            lstm_stage(nc,XT,HT,wx,wh,bias,h0T)
        late=ctx.enter_context(ExitStack())
        w2=late.enter_context(nc.sbuf_tensor("gen_w2",[P,2,3*D*RANK],F32)); w2_in=late.enter_context(semaphores(nc,"prefetch_"))("w2_in")
        ffn0_stage(nc,XT,HT,*[a["L0_ffn_"+n] for n in ("Wq","bq","Wk","bk","Wv","bv","Wr","br","Wo","bo")],ident,g_dram,i_dram,[(w2[:,k],a["L1_cond_W2"][k*P:(k+1)*P,0:3*D*RANK]) for k in range(2)],w2_in)
        cond1_stage(nc,XT,HT,a["cond_1024"],a["L1_cond_base_upT"],*[a["L1_cond_"+n] for n in ("base_down","ln_gamma","ln_beta","W1","bias1")],w2,w2_in,a["L1_cond_W2"],a["L1_cond_bias2"],a["L1_attn_norm_weight"],ident)
        late.close()
        attention_stage(nc,XT,HT,a["L1_attn_w_qkvT"],a["L1_attn_w_outT"],a["L1_attn_memory_keys"],a["L1_attn_memory_values"],a["rope"],ident)
        rnn_stage(nc,XT,HT,a["L1_cond2_Wx"],a["L1_cond2_Wh"],a["L1_cond2_b"],h0T)
        moe_stage(nc,XT,HT,*[a["L1_ffn_"+n] for n in ("gate_w","gate_b","shared_wg","shared_wu","shared_wd","experts_wg","experts_wu","experts_wd")],ident,out)


_AS_THEY_ARE=["x","cond_1024","L0_attn_adj_cols","L0_attn_wq","L0_attn_wk","L0_attn_wv_w","L0_attn_wv_b","L0_attn_qkv_w","L0_attn_out_w","L0_attn_out_b",
    "L0_cond2_Wx","L0_cond2_Wh","L0_cond2_b","L0_ffn_Wq","L0_ffn_bq","L0_ffn_Wk","L0_ffn_bk","L0_ffn_Wv","L0_ffn_bv","L0_ffn_Wr","L0_ffn_br","L0_ffn_Wo","L0_ffn_bo",
    "L1_cond_base_down","L1_cond_ln_gamma","L1_cond_ln_beta","L1_cond_W1","L1_cond_bias1","L1_cond_W2","L1_cond_bias2","L1_attn_norm_weight",
    "L1_cond2_Wx","L1_cond2_Wh","L1_cond2_b","L1_ffn_gate_w","L1_ffn_gate_b","L1_ffn_shared_wg","L1_ffn_shared_wu","L1_ffn_shared_wd","L1_ffn_experts_wg","L1_ffn_experts_wu","L1_ffn_experts_wd"]
def kernel(**inputs):
    import numpy as _np
    import concourse.bacc as _bacc
    from concourse import mybir as _mybir
    from concourse.bass_utils import run_bass_kernel_spmd as _run

    given={n: _np.asarray(v) for n,v in inputs.items()}
    laid={n: given[n] for n in _AS_THEY_ARE}
    laid["xT"]=given["x"].transpose(2,0,1).reshape(2,P,NB,T).transpose(1,0,2,3)
    laid["condT"]=given["cond_1024"].T.reshape(2,P,NB).transpose(1,0,2)
    laid["L0_cond_weightT"]=given["L0_cond_weight"][0,:,:,0].T
    laid["L0_attn_taps"]=given["L0_attn_conv_w"][:,0,::-1,0]
    laid["adj_rowsT"]=given["L0_attn_adj_rows"].reshape(ECH,P).T
    laid["adj_valsT"]=given["L0_attn_adj_vals"].reshape(ECH,P).T
    laid["L1_cond_base_upT"]=given["L1_cond_base_up"].T
    laid["L1_attn_w_qkvT"]=given["L1_attn_w_qkv"].T
    laid["L1_attn_w_outT"]=given["L1_attn_w_out"].T
    memory=given["L1_attn_persist_mem"].reshape(PAIRS,2,PM,DH)
    laid["L1_attn_memory_keys"]=memory.transpose(1,3,0,2).reshape(P,PAIRS,PM)
    laid["L1_attn_memory_values"]=memory.transpose(2,0,1,3)
    laid["rope"]=rope_table()
    nc=_bacc.Bacc("TRN2", target_bir_lowering=False, num_devices=1)
    arrays,aps={},{}
    for n,v in laid.items():
        v=_np.ascontiguousarray(v)
        arrays[f"in_{n}_dram"]=v
        aps[n]=nc.dram_tensor(f"in_{n}_dram",v.shape,_mybir.dt.from_np(v.dtype),kind="ExternalInput").ap()
    out=nc.dram_tensor("out_0_dram",(NB,T,D),_mybir.dt.float32,kind="ExternalOutput").ap()
    build(nc,aps,out)
    r=_run(nc,[arrays],core_ids=[0])
    return r.results[0]["out_0_dram"]
```
